# Optimizing a Trainium2 kernel written in Bass

```python
import numpy as np
import jax
import jax.numpy as jnp

def _softmax(x, axis=-1):
    return jax.nn.softmax(x, axis=axis)

def _gelu(x):
    return jax.nn.gelu(x, approximate=True)

def _silu(x):
    return jax.nn.silu(x)

def _sigmoid(x):
    return jax.nn.sigmoid(x)

def _layernorm(x, axis=-1, eps=1e-05):
    m = jnp.mean(x, axis=axis, keepdims=True)
    v = jnp.var(x, axis=axis, keepdims=True)
    return (x - m) / jnp.sqrt(v + eps)

def _scatter_add(tgt, idx, src, axis=0):
    return tgt.at[idx].add(src)

def _segment_sum(src, seg, n):
    return jax.ops.segment_sum(src, seg, n)
kernel_name = 'mk_gnn_resnorm_d2_gnn_r8_eb7a29'

def setup_inputs(seed: int=0):
    np.random.seed(seed)
    _w = jnp.asarray

    def _rec_inputs():
        import jax
        import jax.numpy as jnp
        _gk = jax.random.key(seed)
        x = -0.000202 + 1 * jax.random.normal(jax.random.fold_in(_gk, 1), (6250, 64), jnp.float32)
        _s = jax.random.randint(jax.random.fold_in(_gk, 2), (100000,), 0, 6250, jnp.int32)
        _d = jax.random.randint(jax.random.fold_in(_gk, 3), (100000,), 0, 6250, jnp.int32)
        _loop = jnp.arange(6250, dtype=jnp.int32)
        src = jnp.concatenate([_s, _d, _loop])
        dst = jnp.concatenate([_d, _s, _loop])
        _o = jnp.argsort(dst, stable=True)
        src = src[_o]
        dst = dst[_o]
        edge_attr_64 = -8.16379e-05 + 0.999858 * jax.random.normal(jax.random.fold_in(_gk, 12), (206250, 64), jnp.float32)
        edge_attr_64_n2 = -8.16379e-05 + 0.999858 * jax.random.normal(jax.random.fold_in(_gk, 13), (206250, 64), jnp.float32)
        edge_attr_64_n3 = -8.16379e-05 + 0.999858 * jax.random.normal(jax.random.fold_in(_gk, 14), (206250, 64), jnp.float32)
        return (x, src, dst, edge_attr_64, edge_attr_64_n2, edge_attr_64_n3)
    x, src, dst, edge_attr_64, edge_attr_64_n2, edge_attr_64_n3 = _rec_inputs()

    def _L0_gnn_setup():
        import jax, jax.numpy as jnp
        import numpy as np
        N_NODES = 12500
        N_EDGES = 200000
        D = 64

        def _segment_mean(data, segment_ids, num_segments):
            num = jax.ops.segment_sum(data, segment_ids, num_segments=num_segments)
            den = jax.ops.segment_sum(jnp.ones_like(data), segment_ids, num_segments=num_segments)
            return num / (1e-06 + den)
        key = jax.random.key(seed)
        ks = jax.random.split(key, 10)
        s = 1.0 / np.sqrt(D)
        return {'node_emb': jax.random.normal(ks[0], (N_NODES, D), jnp.float32), 'edge_emb': jax.random.normal(ks[1], (N_EDGES, D), jnp.float32), 'W1_msg': jax.random.normal(ks[2], (3 * D, D), jnp.float32) * s, 'b1_msg': jnp.zeros((D,), jnp.float32), 'W2_msg': jax.random.normal(ks[3], (D, D), jnp.float32) * s, 'b2_msg': jnp.zeros((D,), jnp.float32), 'W1_upd': jax.random.normal(ks[4], (2 * D, D), jnp.float32) * s, 'b1_upd': jnp.zeros((D,), jnp.float32), 'W2_upd': jax.random.normal(ks[5], (D, D), jnp.float32) * s, 'b2_upd': jnp.zeros((D,), jnp.float32), 'senders': jax.random.randint(ks[6], (N_EDGES,), 0, N_NODES), 'receivers': jax.random.randint(ks[7], (N_EDGES,), 0, N_NODES)}
    _L0_gnn_all = _L0_gnn_setup()
    _L0_gnn_in = {k: v for k, v in _L0_gnn_all.items() if k in ('W1_msg', 'b1_msg', 'W2_msg', 'b2_msg', 'W1_upd', 'b1_upd', 'W2_upd', 'b2_upd')}
    del _L0_gnn_all

    def _L1_gnn_setup():
        import jax, jax.numpy as jnp
        import numpy as np
        N_NODES = 12500
        N_EDGES = 62500
        D_NODE = 64
        D_EDGE = 64
        D_TIME = 64
        D_OUT = 64
        key = jax.random.key(seed)
        ks = jax.random.split(key, 10)
        key_dim = D_NODE + D_TIME + D_EDGE
        m2_dim = D_NODE + D_TIME + D_OUT
        return {'node_feature': jax.random.normal(ks[0], (N_NODES, D_NODE), jnp.float32), 'edge_index': jax.random.randint(ks[1], (N_EDGES, 2), 0, N_NODES, jnp.int64), 'edge_feature': jax.random.normal(ks[2], (N_EDGES, D_EDGE), jnp.float32), 'src_time_features': jax.random.normal(ks[3], (N_EDGES, D_TIME), jnp.float32), 'edge_time': jax.random.normal(ks[4], (N_EDGES, D_TIME), jnp.float32), 'W1': jax.random.normal(ks[5], (D_OUT, key_dim), jnp.float32) / np.sqrt(key_dim), 'b1': jnp.zeros((D_OUT,), jnp.float32), 'W2': jax.random.normal(ks[6], (D_OUT, m2_dim), jnp.float32) / np.sqrt(m2_dim), 'b2': jnp.zeros((D_OUT,), jnp.float32)}
    _L1_gnn_all = _L1_gnn_setup()
    _L1_gnn_in = {k: v for k, v in _L1_gnn_all.items() if k in ('W1', 'b1', 'W2', 'b2')}
    del _L1_gnn_all
    return {'x': x, 'src': src, 'dst': dst, 'edge_attr_64': edge_attr_64, 'edge_attr_64_n2': edge_attr_64_n2, 'edge_attr_64_n3': edge_attr_64_n3, 'L0_gnn_W1_msg': _L0_gnn_in['W1_msg'], 'L0_gnn_b1_msg': _L0_gnn_in['b1_msg'], 'L0_gnn_W2_msg': _L0_gnn_in['W2_msg'], 'L0_gnn_b2_msg': _L0_gnn_in['b2_msg'], 'L0_gnn_W1_upd': _L0_gnn_in['W1_upd'], 'L0_gnn_b1_upd': _L0_gnn_in['b1_upd'], 'L0_gnn_W2_upd': _L0_gnn_in['W2_upd'], 'L0_gnn_b2_upd': _L0_gnn_in['b2_upd'], 'L1_gnn_W1': _L1_gnn_in['W1'], 'L1_gnn_b1': _L1_gnn_in['b1'], 'L1_gnn_W2': _L1_gnn_in['W2'], 'L1_gnn_b2': _L1_gnn_in['b2']}

def reference(x, src, dst, edge_attr_64, edge_attr_64_n2, edge_attr_64_n3, L0_gnn_W1_msg, L0_gnn_b1_msg, L0_gnn_W2_msg, L0_gnn_b2_msg, L0_gnn_W1_upd, L0_gnn_b1_upd, L0_gnn_W2_upd, L0_gnn_b2_upd, L1_gnn_W1, L1_gnn_b1, L1_gnn_W2, L1_gnn_b2):
    import jax
    import jax.numpy as jnp

    def _L0_gnn_ref(node_emb, edge_emb, W1_msg, b1_msg, W2_msg, b2_msg, W1_upd, b1_upd, W2_upd, b2_upd, senders, receivers):
        import jax, jax.numpy as jnp
        import numpy as np
        N_NODES = 12500
        N_EDGES = 200000
        D = 64

        def _segment_mean(data, segment_ids, num_segments):
            num = jax.ops.segment_sum(data, segment_ids, num_segments=num_segments)
            den = jax.ops.segment_sum(jnp.ones_like(data), segment_ids, num_segments=num_segments)
            return num / (1e-06 + den)
        sender_emb = node_emb[senders]
        receiver_emb = node_emb[receivers]
        msg_in = jnp.concatenate([edge_emb, sender_emb, receiver_emb], axis=-1)
        h = jax.nn.silu(msg_in @ W1_msg + b1_msg)
        edge_messages = h @ W2_msg + b2_msg
        node_messages = _segment_mean(edge_messages, receivers, node_emb.shape[0])
        upd_in = jnp.concatenate([node_emb, node_messages], axis=-1)
        hu = jax.nn.silu(upd_in @ W1_upd + b1_upd)
        new_node_emb = hu @ W2_upd + b2_upd
        return new_node_emb

    def _L1_gnn_ref(node_feature, edge_index, edge_feature, src_time_features, edge_time, W1, b1, W2, b2):
        import jax, jax.numpy as jnp
        import numpy as np
        N_NODES = 12500
        N_EDGES = 62500
        D_NODE = 64
        D_EDGE = 64
        D_TIME = 64
        D_OUT = 64
        N = node_feature.shape[0]
        ei = jnp.concatenate([edge_index, edge_index[:, ::-1]], axis=0)
        ef = jnp.concatenate([edge_feature, edge_feature], axis=0)
        stf = jnp.concatenate([src_time_features, src_time_features], axis=0)
        et = jnp.concatenate([edge_time, edge_time], axis=0)
        time_unit = src_time_features[0:1]
        node_id = jnp.arange(N, dtype=ei.dtype)
        ei = jnp.concatenate([ei, jnp.stack([node_id, node_id], axis=1)], axis=0)
        ef = jnp.concatenate([ef, jnp.zeros((N, ef.shape[1]), ef.dtype)], axis=0)
        stf = jnp.concatenate([stf, jnp.tile(time_unit, (N, 1))], axis=0)
        et = jnp.concatenate([et, jnp.tile(time_unit, (N, 1))], axis=0)
        node_i = ei[:, 0]
        node_j = ei[:, 1]
        src_vec = jnp.concatenate([node_feature[node_i], stf], axis=1)
        seg_sum = jax.ops.segment_sum(src_vec, node_i, num_segments=N)
        cnt = jax.ops.segment_sum(jnp.ones((node_i.shape[0], 1), src_vec.dtype), node_i, num_segments=N)
        source_node_vec = seg_sum / jnp.maximum(cnt, 1.0)
        target_vec = jnp.concatenate([node_feature[node_j], ef, et], axis=1)
        neighbor_emb = target_vec @ W1.T + b1
        neighbors_sum = jax.nn.relu(jax.ops.segment_sum(neighbor_emb, node_i, num_segments=N))
        out = jnp.concatenate([neighbors_sum, source_node_vec], axis=1) @ W2.T + b2
        return out
    edge_index_t = jnp.stack([src, dst], axis=1)
    x = _layernorm(x + _L0_gnn_ref(x, edge_attr_64, L0_gnn_W1_msg, L0_gnn_b1_msg, L0_gnn_W2_msg, L0_gnn_b2_msg, L0_gnn_W1_upd, L0_gnn_b1_upd, L0_gnn_W2_upd, L0_gnn_b2_upd, src, dst), axis=-1)
    x = _layernorm(x + _L1_gnn_ref(x, edge_index_t, edge_attr_64, edge_attr_64_n2, edge_attr_64_n3, L1_gnn_W1, L1_gnn_b1, L1_gnn_W2, L1_gnn_b2), axis=-1)
    return x

_drawn_inputs = setup_inputs


def setup_inputs(seed=0):
    import zlib

    import numpy as np

    out = dict(_drawn_inputs(seed))
    spreads = {'L0_gnn_b1_msg': (0.0, 0.1),
     'L0_gnn_b2_msg': (0.0, 0.1),
     'L0_gnn_b1_upd': (0.0, 0.1),
     'L0_gnn_b2_upd': (0.0, 0.1),
     'L1_gnn_b1': (0.0, 0.1),
     'L1_gnn_b2': (0.0, 0.635)}
    factors = {}
    for name, (base, spread) in spreads.items():
        noise = np.random.default_rng([zlib.crc32(name.encode()), seed]).standard_normal(out[name].shape)
        drawn = base * np.exp(spread * noise) if base else spread * noise
        out[name] = jnp.asarray(drawn.astype(out[name].dtype))
    for name, factor in factors.items():
        out[name] = (out[name] * factor).astype(out[name].dtype)
    return out
```

```python
from contextlib import ExitStack

import numpy as np

import concourse.bass as bass
from concourse import mybir

F32 = mybir.dt.float32
BF16 = mybir.dt.bfloat16
I32 = mybir.dt.int32
ALU = mybir.AluOpType
ACT = mybir.ActivationFunctionType
AX = mybir.AxisListType.X

P = 128
N = 6250
E = 206250
D = 64
NB = -(-N // P)
NROWS = (NB + 1) * P
T = 30
LOT = P * T
NL = -(-E // LOT)
NLX = NL + 2
NT = NB + 1
SELF = NB
CH = 5
KB = 7
NC_ = NT // CH
BC = 2 * NC_
BODIES = NL // 2
W = 3 * D + 1
G0 = D + 1
WH = G0 + W
GROUPS = ((0, 2), (2, 2), (4, 1))
NG = len(GROUPS)
SUMMED = [(c, g) for c in range(BC) for g in range(NG) if (c % NC_, g) != (NC_ - 1, NG - 1)]
MAXSW = NB + T + 1
RG = 5
RO = 4
RT = 4
LAG = CH + 2
FAR = 8192.0
assert NT % CH == 0 and NB % KB == 0 and NL % 2 == 0 and BC * CH % RT == 0 and NT % 2 == 0

PARTS = 3
D3 = PARTS * D

WA, WB, WC, W2M, U1A, U1B, W2U, V1A, V1B, V1C, Z2A, Z2B, Z2C = range(13)
B1M, B2M, B1U, B2U, C1, C2, TU = range(7)


def previous_user(c, ring):
    if c >= ring:
        return c - ring
    last = [u for u in range(BC) if u % ring == c % ring][-1]
    return last - BC


def slot_uses(c, ring):
    uses = [u for u in range(BC) if u % ring == c % ring]
    return uses.index(c) + 1, len(uses)


class Count:

    def __init__(self, sem, body, extra=0, credit=0, sweep_bodies=BODIES):
        self.sem, self.body, self.credit = sem, body, credit
        self.sweep = body * sweep_bodies + extra

    def at(self, s, i, n):
        return s * self.sweep + i * self.body + (n + self.credit)


def gnn_kernel(nc, edges, src_t, dst_t, x_t, x_rows, wts, bias, out):
    ctx = ExitStack()
    with ctx:
        def sb(name, shape, dt=F32, c=ctx):
            return c.enter_context(nc.sbuf_tensor(name, shape, dt))

        def sem(name):
            return ctx.enter_context(nc.semaphore(name))

        xd_dram = nc.dram_tensor("xd_dram", (NROWS, 2 * D3), BF16, kind="Internal").ap()
        acc1_dram = nc.dram_tensor("acc1_dram", (NROWS, WH), F32, kind="Internal").ap()
        acc2_dram = nc.dram_tensor("acc2_dram", (NROWS, D), F32, kind="Internal").ap()
        y_dram = nc.dram_tensor("y_dram", (NROWS, D3), BF16, kind="Internal").ap()
        x1_dram = nc.dram_tensor("x1_dram", (NB * P, D), F32, kind="Internal").ap()
        keys_dram = nc.dram_tensor("keys_dram", (MAXSW * NL * P, 2 * NT), BF16, kind="Internal").ap()
        base_dram = nc.dram_tensor("base_dram", (MAXSW, NL), I32, kind="Internal").ap()

        bank = [ctx.enter_context(nc.psum_tensor(f"bank{b}", [P, 512], F32)) for b in range(8)]

        w = sb("w", [D, 13 * D])
        bb = sb("bb", [P, 7, D])
        ident = sb("ident", [P, P])
        ones = sb("ones", [P, P])
        iota_m = sb("iota_m", [P, P])
        iota_bf = sb("iota_bf", [P, P], BF16)
        src_sum = sb("src_sum", [P, NB, W])
        table = sb("table", [P, NB, PARTS, D], BF16)
        ctl = sb("ctl", [1, 4], I32)

        def wt(n):
            return w[:, n * D:(n + 1) * D]

        s_in = sem("s_in")
        s_c = sem("s_c")
        s_v0 = sem("s_v0")
        s_p0 = sem("s_p0")
        s_e0 = sem("s_e0")
        s_o0 = sem("s_o0")
        s_cv = sem("s_cv")
        s_xd = sem("s_xd")
        s_split = sem("s_split")

        sweep_ctx = ExitStack()
        hi = sb("hi", [P, NLX, T], c=sweep_ctx)
        dstf = sb("dstf", [P, NLX, T], c=sweep_ctx)
        rem = sb("rem", [P, NLX, T], c=sweep_ctx)
        lo1 = sb("lo1", [P, NLX, T], BF16, c=sweep_ctx)
        tri = sb("tri", [P, P], BF16, c=sweep_ctx)
        iota_b1 = sb("iota_b1", [P, NT], c=sweep_ctx)
        iota_p = sb("iota_p", [P, 1], c=sweep_ctx)
        iota_j = sb("iota_j", [P, T], BF16, c=sweep_ctx)
        lot0 = sb("lot0", [P, NLX], c=sweep_ctx)
        loops = sb("loops", [P, NLX, T], BF16, c=sweep_ctx)
        scanmask = sb("scanmask", [P, NT, T], BF16, c=sweep_ctx)

        with ExitStack() as c0:
            srci = sb("srci", [P, NLX * T], I32, c=c0)
            dsti = sb("dsti", [P, NLX * T], I32, c=c0)
            tmpi = sb("tmpi", [P, NLX * T], I32, c=c0)
            itmp = sb("itmp", [P, P], I32, c=c0)
            ibt = sb("ibt", [P, NT], I32, c=c0)
            ipt = sb("ipt", [P, 1], I32, c=c0)
            ijt = sb("ijt", [P, T], I32, c=c0)
            ilt = sb("ilt", [P, NLX], I32, c=c0)
            xt = sb("xt", [D, NROWS], c=c0)
            xdb = sb("xdb", [P, NB + 1, 2, D], c=c0)
            xparts = sb("xparts", [P, NB + 1, 2, PARTS, D], BF16, c=c0)
            other = sb("other", [P, NLX * T], c=c0)
            zero = src_sum[:, :, :].rearrange("p b f -> p (b f)")
            block = c0.enter_context(nc.Block())
            NE0 = (NB + 1) // CH
            SH = 7
            assert P == 1 << SH

            @block.sync
            def _(sp):
                sp.dma_start(srci[:, :], src_t).then_inc(s_in, 16)
                sp.dma_start(dsti[:, :], dst_t).then_inc(s_in, 16)
                sp.dma_start(xt[:, :], x_t).then_inc(s_in, 16)
                sp.dma_start(w[:, :], wts).then_inc(s_in, 16)
                sp.dma_start(bb[:, :, :].rearrange("p a d -> p (a d)"),
                             bias.to_broadcast([P, 7 * D])).then_inc(s_in, 16)
                sp.wait_ge(s_c, 1)
                a1 = acc1_dram.rearrange("(p r) c -> p (r c)", p=P)
                for q in range(5):
                    sp.dma_start(a1[:, q * 10 * WH:(q + 1) * 10 * WH], zero[:, 0:10 * WH]).then_inc(s_o0, 16)
                a2 = acc2_dram.rearrange("(p r) c -> p (r c)", p=P)
                yz = y_dram.rearrange("(p r) c -> p (r c)", p=P)
                ky = (NB + 1) * D3 // 2
                for q in range(2):
                    k = (NB + 1) * D // 2
                    sp.dma_start(a2[:, q * k:(q + 1) * k], zero[:, 0:k]).then_inc(s_o0, 16)
                    sp.dma_start(yz[:, q * ky:(q + 1) * ky], zero[:, 0:ky // 2].bitcast(BF16)).then_inc(s_o0, 16)
                sp.wait_ge(s_split, 2)
                sp.dma_start(xd_dram.rearrange("(b p) d -> p b d", p=P),
                             xparts[:, :, :, :, :].rearrange("p b m a d -> p b (m a d)")).then_inc(s_xd, 16)
                sp.wait_ge(s_o0, 16 * 9)
                sp.wait_ge(s_xd, 16)

            @block.gpsimd
            def _(pool):
                pool.memset(src_sum[:, :, :], 0.0).then_inc(s_c, 1)
                pool.memset(ident[:, :], 0.0).then_inc(s_c, 1)
                pool.memset(ones[:, :], 1.0).then_inc(s_c, 1)
                pool.memset(tri[:, :], 1.0).then_inc(s_c, 1)
                pool.memset(scanmask[:, :, :], 1.0).then_inc(s_c, 1)
                pool.wait_ge(s_c, 5)
                pool.affine_select(out=ident[:, :], in_=ident[:, :], compare_op=ALU.not_equal, fill=1.0,
                                   base=0, pattern=[[-1, P]], channel_multiplier=1).then_inc(s_c, 1)
                pool.affine_select(out=tri[:, :], in_=tri[:, :], compare_op=ALU.is_gt, fill=0.0,
                                   base=0, pattern=[[1, P]], channel_multiplier=-1).then_inc(s_c, 1)
                pool.memset(scanmask[:, :, 0:1], 0.0).then_inc(s_c, 1)
                pool.iota(itmp[:, :], pattern=[[1, P]], base=0, channel_multiplier=0).then_inc(s_c, 1)
                pool.iota(ibt[:, :], pattern=[[1, NT]], base=1, channel_multiplier=0).then_inc(s_c, 1)
                pool.iota(ipt[:, :], pattern=[[1, 1]], base=0, channel_multiplier=1).then_inc(s_c, 1)
                pool.iota(ijt[:, :], pattern=[[1, T]], base=0, channel_multiplier=0).then_inc(s_c, 1)
                pool.iota(ilt[:, :], pattern=[[LOT, NLX]], base=0, channel_multiplier=0).then_inc(s_c, 1)
                pool.wait_ge(s_c, 13)
                pool.tensor_copy(iota_m[:, :], itmp[:, :]).then_inc(s_cv, 1)
                pool.tensor_copy(iota_bf[:, :], itmp[:, :]).then_inc(s_cv, 1)
                pool.tensor_copy(iota_b1[:, :], ibt[:, :]).then_inc(s_cv, 1)
                pool.tensor_copy(iota_p[:, :], ipt[:, :]).then_inc(s_cv, 1)
                pool.tensor_copy(iota_j[:, :], ijt[:, :]).then_inc(s_cv, 1)
                pool.tensor_copy(lot0[:, :], ilt[:, :]).then_inc(s_cv, 1)
                pool.wait_ge(s_cv, 6)

            @block.tensor
            def _(pe):
                pe.wait_ge(s_in, 80)
                for e in range(NE0):
                    if e >= 2:
                        pe.wait_ge(s_e0, e - 1)
                    for k in range(CH):
                        b = e * CH + k
                        lhs = xt[:, b * P:(b + 1) * P]
                        pe.matmul(bank[e % 2][:, k * D:(k + 1) * D], lhs, wt(WB), start=True, stop=True)
                        last = pe.matmul(bank[2 + e % 2][:, k * D:(k + 1) * D], lhs, wt(WC), start=True, stop=True)
                    last.then_inc(s_p0, 1)

            @block.vector
            def _(dve):
                done = [0]

                def step(ins):
                    ins.then_inc(s_v0, 1)
                    done[0] += 1
                    dve.wait_ge(s_v0, done[0])

                for e in range(NE0):
                    dve.wait_ge(s_p0, e + 1)
                    b0 = e * CH
                    nd = CH
                    snd = bank[e % 2][:, 0:nd * D].rearrange("p (k d) -> p k d", d=D)
                    dve.tensor_copy(xdb[:, b0:b0 + nd, 1, :], snd)
                    dve.tensor_tensor(xdb[:, b0:b0 + nd, 0, :],
                                      bank[2 + e % 2][:, 0:nd * D].rearrange("p (k d) -> p k d", d=D),
                                      bb[:, B1M:B1M + 1, :].to_broadcast([P, nd, D]), ALU.add).then_inc(s_e0, 1)
                dve.wait_ge(s_e0, NE0)
                for a in range(PARTS):
                    step(dve.tensor_copy(xparts[:, :, :, a, :], xdb[:, :, :, :]))
                    if a < PARTS - 1:
                        step(dve.tensor_tensor(xdb[:, :, :, :], xdb[:, :, :, :], xparts[:, :, :, a, :], ALU.subtract))
                dve.sem_inc(s_split, 2)
                step(dve.tensor_copy(table[:, :, :, :].rearrange("p b a d -> p b (a d)"),
                                     xparts[:, 0:NB, 1, :, :].rearrange("p b a d -> p b (a d)")))
                f = "p l t -> p (l t)"
                def flat(v):
                    return v[:, :, :].rearrange(f)

                step(dve.tensor_copy(flat(hi), srci[:, :]))
                step(dve.tensor_scalar(flat(rem), flat(hi), float(NB * P) - 0.5, None, ALU.is_lt))
                step(dve.tensor_copy(flat(dstf), dsti[:, :]))
                step(dve.tensor_tensor(flat(loops), flat(hi), flat(dstf), ALU.is_equal))
                step(dve.tensor_tensor(other[:, :], flat(hi), flat(dstf), ALU.not_equal))
                step(dve.tensor_scalar(tmpi[:, :], srci[:, :], SH, None, ALU.arith_shift_right))
                step(dve.tensor_scalar(dsti[:, :], srci[:, :], P - 1, None, ALU.bitwise_and))
                step(dve.tensor_copy(flat(hi), tmpi[:, :]))
                step(dve.scalar_tensor_tensor(flat(hi), flat(hi), -float(SELF), other[:, :], ALU.add, ALU.mult))
                step(dve.tensor_scalar(flat(hi), flat(hi), float(SELF), None, ALU.add))
                step(dve.scalar_tensor_tensor(flat(lo1), dsti[:, :], 1.0, other[:, :], ALU.add, ALU.mult))
                step(dve.memset(ctl[:, :], 0))

        gh_ready = [sem(f"gh_ready{r}") for r in range(RG)]
        gh_use = {}
        for c in range(BC):
            gh_use[c] = slot_uses(c, RG)
        gh_count = [Count(gh_ready[r], 16 * CH * len([c for c in range(BC) if c % RG == r])) for r in range(RG)]
        idx_ready = Count(sem("idx_ready"), 2, extra=2, credit=4)
        oh_ready = Count(sem("oh_ready"), BC)
        copied = Count(sem("copied"), BC * CH, credit=4)
        h_ready = Count(sem("h_ready"), BC, credit=4)
        trans = Count(sem("trans"), BC * CH)
        pre_done = Count(sem("pre_done"), BC, credit=BC)
        srcsum_ready = Count(sem("srcsum_ready"), len(SUMMED))
        srcsum_added = Count(sem("srcsum_added"), len(SUMMED), credit=4)
        dst_summed = Count(sem("dst_summed"), BC, credit=BC)
        dwin_saved = Count(sem("dwin_saved"), 2, extra=1, credit=4)
        dwin_added = Count(sem("dwin_added"), 32, extra=16, credit=16)
        xdw_ready = [Count(sem(f"xdw_ready{q}"), 16) for q in range(2)]
        keys_saved = [Count(sem(f"keys_saved{q}"), 16, credit=32) for q in range(2)]
        count_ready = Count(sem("count_ready"), 2, extra=2)
        prefix_done = Count(sem("prefix_done"), 2, extra=2)
        spread_ready = Count(sem("spread_ready"), 2, extra=2)
        inverted = Count(sem("inverted"), 2, extra=2)
        base_min = Count(sem("base_min"), 0, extra=1)
        base_t = Count(sem("base_t"), 0, extra=1)
        base_col = Count(sem("base_col"), 0, extra=1)
        base_bc = Count(sem("base_bc"), 0, extra=1)
        base_set = Count(sem("base_set"), 0, extra=1)
        base_saved = Count(sem("base_saved"), 0, extra=16, credit=16)
        left_ready = Count(sem("left_ready"), 0, extra=1)
        left_total = Count(sem("left_total"), 0, extra=1)
        sweep_end = Count(sem("sweep_end"), 0, extra=1)
        s_pass = sem("s_pass")
        s_chain = sem("s_chain")

        def wait(eng, cnt, s, i, n):
            eng.wait_ge(cnt.sem, cnt.at(s, i, n))

        def hold(eng, cnt, s, i, n):
            eng.wait_ge(cnt.sem, cnt.at(s, i, n))
            eng.sem_inc(s_pass, 1)

        with sweep_ctx, ExitStack() as c1:
            gh = sb("gh", [P, RG, CH, WH], c=c1)
            oh = sb("oh", [P, RO, 2, CH, P], c=c1)
            tcopy = sb("tcopy", [P, RT, 2 * P], BF16, c=c1)
            rcopy = sb("rcopy", [D, RT, P], c=c1)
            onehot_b = sb("onehot_b", [P, NT, T], c=c1)
            run = sb("run", [P, NT, T], c=c1)
            vals = sb("vals", [P, 4, NT, T], BF16, c=c1)
            slot_oh = sb("slot_oh", [P, T, P], BF16, c=c1)
            khi = sb("khi", [P, NLX, T], c=c1)
            dl1 = sb("dl1", [P, NLX, T], BF16, c=c1)
            scratch = vals[:, :, :, :].rearrange("p a b t -> p (a b t)")[:, 0:2 * NLX * T].bitcast(F32)\
                .rearrange("p (l t) -> p l t", t=T)
            inw = slot_oh[:, :, :].rearrange("p a b -> p (a b)")[:, 0:2 * NLX * T].bitcast(F32)\
                .rearrange("p (l t) -> p l t", t=T)
            hist = sb("hist", [P, NT], BF16, c=c1)
            rank = sb("rank", [P, T], c=c1)
            placed = sb("placed", [P, T], c=c1)
            invs = sb("invs", [P, 2, NT], c=c1)
            idf = sb("idf", [P, NT], c=c1)
            idx = sb("idx", [P, 2, NT], I32, c=c1)
            keys = sb("keys", [P, 2, 2, NT], BF16, c=c1)
            sl1 = sb("sl1", [P, NLX, T], BF16, c=c1)
            xdw = sb("xdw", [P, 2, 2, PARTS, D], BF16, c=c1)
            dwin = sb("dwin", [P, 2, WH], c=c1)
            unread = sb("unread", [P, 2 * D3], BF16, c=c1)
            minp = sb("minp", [P, NLX], c=c1)
            bcol = sb("bcol", [P, 2], c=c1)
            bdiag = sb("bdiag", [NLX, NLX], c=c1)
            base_f = sb("base_f", [P, NLX], c=c1)
            base_i = sb("base_i", [1, NLX + 1], I32, c=c1)
            left = sb("left", [P, 2], c=c1)
            swf = sb("swf", [1, 4], c=c1)
            tb, pb, db, rb, sbk = [bank[0], bank[1]], [bank[2], bank[3]], bank[4], bank[5], [bank[6], bank[7]]
            block = c1.enter_context(nc.Block())

            def sweeps(eng, name):
                end = eng.alloc_register(name)
                eng.reg_mov(end, 1)
                return end

            @block.sync
            def _(sp):
                end = sweeps(sp, "sweep_end_sp")
                for cnt in (idx_ready, copied, h_ready, pre_done, srcsum_added, dst_summed, dwin_saved,
                            keys_saved[0], keys_saved[1], base_saved):
                    sp.sem_inc(cnt.sem, cnt.credit)
                with sp.Fori(0, end) as s:
                    sp.wait_ge(base_set.sem, base_set.at(s, 0, 1))
                    sp.dma_start(base_dram[bass.ds(s, 1), :], base_i[0:1, 1:1 + NL]).then_inc(base_saved.sem, 16)
                    with sp.Fori(0, BODIES) as i:
                        for q in range(2):
                            b = sp.value_load(base_i[0:1, bass.ds(i * 2 + (1 + q), 1)], min_val=0, max_val=N - 1)
                            hold(sp, pre_done, s, i, NC_ * (q + 1) - BC)
                            sp.dma_start(xdw[:, q, :, :, :].rearrange("p m a d -> p (m a d)"), xd_dram[bass.ds(b, P), :]).then_inc(xdw_ready[q].sem, 16)
                            hold(sp, idx_ready, s, i, q + 1)
                            sp.dma_start(keys_dram[bass.ds((s * NL + i * 2 + q) * P, P), :],
                                         keys[:, q, :, :].rearrange("p a b -> p (a b)")).then_inc(keys_saved[q].sem, 16)
                    hold(sp, sweep_end, s, 0, 1)
                    sp.load(end, ctl[0:1, 0:1])
                    hold(sp, base_saved, s, 0, 16)

            @block.gpsimd
            def _(pool):
                end = sweeps(pool, "sweep_end_pool")
                pool.memset(gh[:, :, :, D:G0], 1.0).then_inc(s_c, 1)
                pool.memset(gh[:, :, :, WH - 1:WH], 1.0).then_inc(s_c, 1)
                pool.dma_start(unread[:, :], xd_dram[0:P, :]).then_inc(dwin_added.sem, 16)
                pool.wait_ge(s_c, 15)

                def add_window(s, i, q, n):
                    b = pool.value_load(base_i[0:1, bass.ds(i * 2 + q, 1)], min_val=0, max_val=N - 1)
                    hold(pool, dwin_saved, s, i, n + 1)
                    hold(pool, dwin_added, s, i, 16 * n)
                    pool.dma_start(acc1_dram[bass.ds(b, P), :], dwin[:, (q + 1) % 2, :],
                                   accum_op=ALU.add).then_inc(dwin_added.sem, 16)

                with pool.Fori(0, end) as s:
                    hold(pool, base_set, s, 0, 1)
                    with pool.Fori(0, BODIES) as i:
                        for c in range(BC):
                            if c % NC_ == 0:
                                hold(pool, idx_ready, s, i, c // NC_ + 1)
                            hold(pool, dst_summed, s, i, previous_user(c, RG) + 1)
                            for k in range(CH):
                                t = c % NC_ * CH + k
                                pool.indirect_dma_start(
                                    out=gh[:, c % RG, k, G0:G0 + 3 * D], out_offset=None, in_=edges,
                                    in_offset=bass.IndirectOffsetOnAxis(ap=idx[:, c // NC_, t:t + 1], axis=0),
                                ).then_inc(gh_ready[c % RG], 16)
                            if c == 4:
                                add_window(s, i, 0, 0)
                            if c == NC_ + 4:
                                add_window(s, i, 1, 1)
                    add_window(s, BODIES, 0, 0)
                    hold(pool, dwin_added, s, BODIES, 16)
                    hold(pool, sweep_end, s, 0, 1)
                    pool.load(end, ctl[0:1, 0:1])

            @block.scalar
            def _(act):
                end = sweeps(act, "sweep_end_act")
                with act.Fori(0, end) as s:
                    with act.Fori(0, BODIES) as i:
                        for t in range(BC * CH):
                            c, k = t // CH, t % CH
                            act.wait_ge(trans.sem, trans.at(s, i, t + 1))
                            if k == 0:
                                pass
                            act.activation(tcopy[:, t % RT, :], tb[t % 2][:, 0:2 * P], ACT.Copy)
                            act.activation(rcopy[:, t % RT, :], tb[t % 2][0:D, 2 * P:3 * P], ACT.Copy)\
                                .then_inc(copied.sem, 1)
                            if k == CH - 1:
                                act.wait_ge(pre_done.sem, pre_done.at(s, i, c + 1))
                                act.activation(gh[:, c % RG, :, 0:D],
                                               pb[c % 2][:, 0:CH * D].rearrange("p (k d) -> p k d", d=D),
                                               ACT.Silu).then_inc(h_ready.sem, 1)
                    hold(act, sweep_end, s, 0, 1)
                    act.load(end, ctl[0:1, 0:1])

            @block.tensor
            def _(pe):
                end = sweeps(pe, "sweep_end_pe")

                def prefix(s, i, n):
                    wait(pe, count_ready, s, i, n + 1)
                    pe.matmul(rb[:, 0:NT], tri[:, :], hist[:, :], start=True, stop=True).then_inc(prefix_done.sem, 1)

                def invert(s, i, n):
                    wait(pe, spread_ready, s, i, n + 1)
                    for j in range(T):
                        last = pe.matmul(rb[:, 64:64 + 4 * NT], slot_oh[:, j, :],
                                         vals[:, :, :, j].rearrange("p a b -> p (a b)"),
                                         start=(j == 0), stop=(j == T - 1))
                    last.then_inc(inverted.sem, 1)

                with pe.Fori(0, end) as s:
                    hold(pe, base_min, s, 0, 1)
                    pe.transpose(rb[0:NLX, 0:P], minp[:, :], ident[:, :]).then_inc(base_t.sem, 1)
                    wait(pe, base_col, s, 0, 1)
                    pe.matmul(rb[:, 0:NLX], ones[0:NLX, :], bdiag[:, :], start=True, stop=True)\
                        .then_inc(base_bc.sem, 1)
                    for q in range(2):
                        prefix(s, 0, q)
                        invert(s, 0, q)

                    with pe.Fori(0, BODIES) as i:
                        def products(t):
                            c, k = t // CH, t % CH
                            b = t % NT
                            o = pb[c % 2][:, k * D:(k + 1) * D]
                            if k == 0:
                                wait(pe, h_ready, s, i, c - 1)
                            if b == 0:
                                wait(pe, xdw_ready[c // NC_], s, i, 16)
                            wait(pe, copied, s, i, t + 1)
                            tc = tcopy[:, t % RT, :]
                            for a in range(PARTS):
                                senders = xdw[:, c // NC_, 1, a, :] if b == SELF else table[:, b, a, :]
                                pe.matmul(o, tc[:, 0:P], senders, start=(a == 0), stop=False)
                            for a in range(PARTS):
                                pe.matmul(o, tc[:, P:2 * P], xdw[:, c // NC_, 0, a, :], start=False, stop=False)
                            last = pe.matmul(o, rcopy[:, t % RT, :], wt(WA), start=False, stop=True)
                            if k == CH - 1:
                                last.then_inc(pre_done.sem, 1)

                        def dst_sum(t):
                            c, k = t // CH, t % CH
                            b = t % NT
                            if k == 0:
                                wait(pe, h_ready, s, i, c + 1)
                            if b == 0:
                                wait(pe, dwin_saved, s, i, c // NC_ + 1)
                            last = pe.matmul(db[:, 0:WH], oh[:, c % RO, 1, k, :], gh[:, c % RG, k, :],
                                             start=(b == 0), stop=(b == NT - 1))
                            if b == SELF:
                                last = pe.matmul(db[:, G0:WH], oh[:, c % RO, 1, k, :], gh[:, c % RG, k, G0:WH],
                                                 start=False, stop=True, skip_group_check=True)
                            if k == CH - 1:
                                last.then_inc(dst_summed.sem, 1)

                        for q in range(2):
                            for u in range(NT + LAG):
                                t = q * NT + u
                                if u < NT:
                                    c, k = t // CH, t % CH
                                    if k == 0:
                                        wait(pe, oh_ready, s, i, c + 1)
                                        n = gh_use[c][0]
                                        wait(pe, gh_count[c % RG], s, i, 16 * CH * n)
                                    wait(pe, copied, s, i, t - 1)
                                    for m, a in enumerate((oh[:, c % RO, 0, k, :], oh[:, c % RO, 1, k, :],
                                                           gh[:, c % RG, k, G0:G0 + D])):
                                        rows = D if m == 2 else P
                                        last = pe.transpose(tb[t % 2][0:rows, m * P:(m + 1) * P], a, ident[:, :])
                                    last.then_inc(trans.sem, 1)
                                    g = [n for n, (k0, kn) in enumerate(GROUPS) if k0 <= k < k0 + kn][0]
                                    k0, kn = GROUPS[g]
                                    if u != SELF:
                                        n = SUMMED.index((c, g))
                                        if k == k0:
                                            wait(pe, srcsum_added, s, i, n - 1)
                                        last = pe.matmul(sbk[n % 2][:, (k - k0) * W:(k - k0 + 1) * W],
                                                         oh[:, c % RO, 0, k, :], gh[:, c % RG, k, G0:WH],
                                                         start=True, stop=True)
                                        if k == k0 + kn - 1:
                                            last.then_inc(srcsum_ready.sem, 1)
                                if 1 <= u <= NT:
                                    products(t - 1)
                                if u == 3 * CH + 1:
                                    prefix(s, i, 2 + q)
                                if u == 7 * CH + 1:
                                    invert(s, i, 2 + q)
                                if u >= LAG:
                                    dst_sum(t - LAG)
                    wait(pe, left_ready, s, 0, 1)
                    pe.matmul(rb[:, 0:1], ones[:, :], left[:, 0:1], start=True, stop=True).then_inc(left_total.sem, 1)
                    hold(pe, sweep_end, s, 0, 1)
                    pe.load(end, ctl[0:1, 0:1])

            @block.vector
            def _(dve):
                end = sweeps(dve, "sweep_end_dve")
                links = {"pro": 0, "body": 0, "end": 0}
                plan = {"pro": LINKS_PRO, "body": LINKS_BODY, "end": LINKS_END}
                per_sweep = LINKS_PRO + LINKS_BODY * BODIES + LINKS_END

                def link(ins, part, s, i):
                    ins.then_inc(s_chain, 1)
                    links[part] += 1
                    n = links[part] + (plan["pro"] if part != "pro" else 0)
                    if part == "end":
                        n += plan["body"] * BODIES
                    dve.wait_ge(s_chain, s * per_sweep + i * plan["body"] + n)

                def deal_a(part, s, i, l):
                    link(dve.tensor_tensor(onehot_b[:, :, :],
                                           khi[:, bass.ds(l, 1), :].to_broadcast([P, NT, T]),
                                           iota_b1[:, :].unsqueeze(2).to_broadcast([P, NT, T]), ALU.is_equal),
                         part, s, i)
                    with nc.allow_low_precision("counts of at most 30 are exact"):
                        dve.tensor_reduce(hist[:, :], onehot_b[:, :, :], AX, ALU.add).then_inc(count_ready.sem, 1)

                def deal_b(part, s, i, n):
                    link(dve.tensor_copy(run[:, :, :], onehot_b[:, :, :]), part, s, i)
                    wait(dve, prefix_done, s, i, n + 1)
                    link(dve.tensor_tensor(run[:, :, 0:1], run[:, :, 0:1], rb[:, 0:NT].unsqueeze(2), ALU.add),
                         part, s, i)
                    flat = "p b t -> p (b t)"
                    link(dve.tensor_tensor_scan(run[:, :, :].rearrange(flat), scanmask[:, :, :].rearrange(flat),
                                                run[:, :, :].rearrange(flat), 0.0, ALU.mult, ALU.add), part, s, i)
                    link(dve.tensor_tensor(run[:, :, :], run[:, :, :], onehot_b[:, :, :], ALU.mult), part, s, i)
                    link(dve.tensor_reduce(rank[:, :], run[:, :, :].rearrange("p b t -> p t b"), AX, ALU.add),
                         part, s, i)

                def deal_c(part, s, i, l):
                    link(dve.tensor_scalar(placed[:, :], rank[:, :], float(P) + 0.5, None, ALU.is_lt), part, s, i)
                    link(dve.scalar_tensor_tensor(placed[:, :], rank[:, :], 0.5, placed[:, :], ALU.is_gt, ALU.mult),
                         part, s, i)
                    dve.tensor_tensor(rem[:, bass.ds(l, 1), :], rem[:, bass.ds(l, 1), :],
                                      placed[:, :].unsqueeze(1), ALU.subtract)
                    link(dve.tensor_scalar(rank[:, :], rank[:, :], -1.0, None, ALU.add), part, s, i)
                    link(dve.tensor_tensor(slot_oh[:, :, :], rank[:, :].unsqueeze(2).to_broadcast([P, T, P]),
                                           iota_m[:, :].unsqueeze(1).to_broadcast([P, T, P]), ALU.is_equal),
                         part, s, i)

                def deal_d(part, s, i, l):
                    dve.tensor_scalar(vals[:, 0, :, :], onehot_b[:, :, :], iota_p[:, 0:1], None, ALU.mult)
                    dve.tensor_tensor(vals[:, 1, :, :], onehot_b[:, :, :],
                                      iota_j[:, :].unsqueeze(1).to_broadcast([P, NT, T]), ALU.mult)
                    dve.tensor_tensor(vals[:, 2, :, :], onehot_b[:, :, :],
                                      sl1[:, bass.ds(l, 1), :].to_broadcast([P, NT, T]), ALU.mult)
                    dve.tensor_tensor(vals[:, 3, :, :], onehot_b[:, :, :],
                                      dl1[:, bass.ds(l, 1), :].to_broadcast([P, NT, T]),
                                      ALU.mult).then_inc(spread_ready.sem, 1)

                def deal_e(part, s, i, l, q, n):
                    wait(dve, inverted, s, i, n + 1)
                    wait(dve, keys_saved[q], s, i, 16 if n >= 2 else 0)
                    link(dve.tensor_copy(invs[:, :, :], rb[:, 64:64 + 2 * NT].rearrange("p (a b) -> p a b", a=2)),
                         part, s, i)
                    link(dve.scalar_tensor_tensor(idf[:, :], invs[:, 0, :], float(T), invs[:, 1, :],
                                                  ALU.mult, ALU.add), part, s, i)
                    dve.tensor_scalar(idx[:, q, :], idf[:, :], lot0[:, bass.ds(l, 1)], None, ALU.add)
                    link(dve.tensor_scalar(keys[:, q, :, :],
                                           rb[:, 64 + 2 * NT:64 + 4 * NT].rearrange("p (a b) -> p a b", a=2),
                                           -1.0, None, ALU.add), part, s, i)
                    dve.sem_inc(idx_ready.sem, 1)

                def onehots(s, i, c):
                    q, b0 = c // NC_, c % NC_ * CH
                    wait(dve, dst_summed, s, i, previous_user(c, RO) + 1)
                    for m in range(2):
                        last = dve.tensor_tensor(
                            oh[:, c % RO, m, :, :],
                            keys[:, q, m, b0:b0 + CH].unsqueeze(2).to_broadcast([P, CH, P]),
                            iota_m[:, :].unsqueeze(1).to_broadcast([P, CH, P]), ALU.is_equal)
                    last.then_inc(oh_ready.sem, 1)

                def add_group(s, i, c, g):
                    k0, kn = GROUPS[g]
                    b0 = c % NC_ * CH + k0
                    n = SUMMED.index((c, g))
                    wait(dve, srcsum_ready, s, i, n + 1)
                    dve.tensor_tensor(src_sum[:, b0:b0 + kn, :], src_sum[:, b0:b0 + kn, :],
                                      sbk[n % 2][:, 0:kn * W].rearrange("p (k f) -> p k f", f=W),
                                      ALU.add).then_inc(srcsum_added.sem, 1)

                dve.memset(base_i[:, :], 0).then_inc(s_v0, 1)
                dve.memset(swf[:, :], 0.0).then_inc(s_v0, 1)
                dve.wait_ge(s_v0, 14 + 2 * PARTS)
                dve.wait_ge(s_c, 15)
                with dve.Fori(0, end) as s:
                    p0 = ("pro", s, 0)
                    link(dve.scalar_tensor_tensor(khi[:, :, :], dstf[:, :, :], -FAR, rem[:, :, :], ALU.add, ALU.mult), *p0)
                    dve.tensor_reduce(minp[:, :], khi[:, :, :], AX, ALU.min).then_inc(base_min.sem, 1)
                    wait(dve, base_t, s, 0, 1)
                    link(dve.tensor_reduce(bcol[0:NLX, 0:1], rb[0:NLX, 0:P], AX, ALU.min), *p0)
                    link(dve.tensor_scalar(bcol[0:NLX, 1:2], bcol[0:NLX, 0:1], FAR, float(N - 1), ALU.add, ALU.min), *p0)
                    link(dve.tensor_scalar(bdiag[:, :], ident[0:NLX, 0:NLX], bcol[0:NLX, 1:2], None, ALU.mult), *p0)
                    dve.sem_inc(base_col.sem, 1)
                    wait(dve, base_bc, s, 0, 1)
                    wait(dve, base_saved, s, 0, 0)
                    wait(dve, dwin_added, s, 0, 0)
                    dve.memset(dwin[:, 1, :], 0.0).then_inc(dwin_saved.sem, 1)
                    link(dve.tensor_copy(base_f[:, :], rb[:, 0:NLX]), *p0)
                    link(dve.tensor_copy(base_i[0:1, 1:1 + NLX], base_f[0:1, :]), *p0)
                    dve.sem_inc(base_set.sem, 1)
                    link(dve.tensor_tensor(scratch, dstf[:, :, :],
                                           base_f[:, :].unsqueeze(2).to_broadcast([P, NLX, T]), ALU.subtract), *p0)
                    link(dve.tensor_scalar(dl1[:, :, :], scratch, 1.0, None, ALU.add), *p0)
                    link(dve.tensor_tensor(sl1[:, :, :], dl1[:, :, :], loops[:, :, :], ALU.mult), *p0)
                    dve.tensor_tensor(sl1[:, :, :], sl1[:, :, :], lo1[:, :, :], ALU.add)
                    link(dve.scalar_tensor_tensor(inw, scratch, float(P) - 0.5, rem[:, :, :], ALU.is_lt, ALU.mult), *p0)
                    link(dve.scalar_tensor_tensor(khi[:, :, :], hi[:, :, :], 1.0, inw, ALU.add, ALU.mult), *p0)
                    for q in range(2):
                        deal_a(*p0, q)
                        deal_b(*p0, q)
                        deal_c(*p0, q)
                        deal_d(*p0, q)
                        deal_e(*p0, q, q, q)
                    with dve.Fori(0, BODIES) as i:
                        b0 = ("body", s, i)
                        for c in range(BC):
                            q, cc = c // NC_, c % NC_
                            onehots(s, i, c)
                            if cc > 0:
                                for g in range(NG):
                                    add_group(s, i, c - 1, g)
                            nxt = i * 2 + (2 + q)
                            if cc == 1:
                                deal_a(*b0, nxt)
                            if cc == 3:
                                deal_b(*b0, 2 + q)
                            if cc == 4:
                                deal_c(*b0, nxt)
                            if cc == 6:
                                deal_d(*b0, nxt)
                            if cc == NC_ - 1:
                                wait(dve, gh_count[c % RG], s, i, 16 * CH * gh_use[c][0])
                                deal_e(*b0, nxt, q, 2 + q)
                                for g in range(NG - 1):
                                    add_group(s, i, c, g)
                                wait(dve, dst_summed, s, i, c + 1)
                                wait(dve, dwin_added, s, i, 16 * q)
                                dve.tensor_copy(dwin[:, q, :], db[:, 0:WH]).then_inc(dwin_saved.sem, 1)
                    e0 = ("end", s, 0)
                    dve.tensor_reduce(left[:, 0:1], rem[:, :, :].rearrange("p l t -> p (l t)"), AX, ALU.add)\
                        .then_inc(left_ready.sem, 1)
                    link(dve.tensor_scalar(swf[:, 0:1], swf[:, 0:1], 1.0, None, ALU.add), *e0)
                    link(dve.tensor_scalar(swf[:, 1:2], swf[:, 0:1], 1.0, None, ALU.add), *e0)
                    wait(dve, left_total, s, 0, 1)
                    link(dve.tensor_scalar(swf[:, 2:3], rb[0:1, 0:1], 0.5, None, ALU.is_gt), *e0)
                    link(dve.tensor_tensor(swf[:, 2:3], swf[:, 2:3], swf[:, 1:2], ALU.mult), *e0)
                    link(dve.tensor_copy(ctl[0:1, 0:1], swf[:, 2:3]), *e0)
                    link(dve.tensor_copy(ctl[0:1, 1:2], swf[:, 0:1]), *e0)
                    dve.sem_inc(sweep_end.sem, 1)
                    dve.load(end, ctl[0:1, 0:1])
                assert links == plan, links


        src_y = sb("src_y", [P, NB, D])
        y_tab = sb("y_tab", [P, NB, D])
        update_nodes(nc, sb, sem, bank, wt, bb, ident, table, y_tab, src_y, acc1_dram, x_rows, x_t, x1_dram, y_dram)
        sum_neighbours(nc, sb, sem, bank, iota_m, table, src_y, acc2_dram, y_dram, keys_dram, base_dram, ctl)
        finish_nodes(nc, sb, sem, bank, wt, bb, ident, src_sum, y_tab, src_y, acc1_dram, acc2_dram, x1_dram, out)


LINKS_PRO = 11 + 2 * 13
LINKS_BODY = 2 * 13
LINKS_END = 6
HALVES = ((0, 4), (4, 3))


class Turns:

    def __init__(self, sem, passed, names):
        self.sem, self.passed, self.names = sem, passed, names

    def value(self, e, name):
        return e * len(self.names) + (self.names.index(name) + 1)

    def wait_before(self, eng, e, name):
        eng.wait_ge(self.sem, self.value(e, name))
        eng.sem_inc(self.passed, 1)

    def wait_all(self, eng, e):
        eng.wait_ge(self.sem, e * len(self.names) + (len(self.names) + 1))
        eng.sem_inc(self.passed, 1)


def node_rows(dram, e):
    return dram[bass.ds(e * (KB * P), KB * P), :].rearrange("(k p) c -> p k c", p=P)


def transpose_blocks(pe, bank, src, ident):
    for h, (k0, kn) in enumerate(HALVES):
        for k in range(kn):
            last = pe.transpose(bank[1 + h][0:D, k * P:(k + 1) * P], src(k0 + k), ident[:, :])
    return last


def multiply_blocks(pe, bank, terms):
    for k in range(KB):
        for n, (lhs, weight) in enumerate(terms):
            last = pe.matmul(bank[0][:, k * D:(k + 1) * D], lhs[:, k * P:(k + 1) * P], weight,
                             start=(n == 0), stop=(n == len(terms) - 1))
    return last


def copy_blocks(dve, bank, dst):
    for h, (k0, kn) in enumerate(HALVES):
        last = dve.tensor_copy(dst[:, k0 * P:(k0 + kn) * P], bank[1 + h][0:D, 0:kn * P])
    return last


UPDATE_STEPS = ("sumh_t", "sumh_c", "msg", "cnt", "rcnt", "b2cnt", "num", "mean", "mean_t", "mean_c", "upd1",
                "pre", "silu", "hu_t", "hu_c", "upd2", "new", "res", "ln_sum", "ln_mean", "ln_cen", "ln_sq", "ln_var",
                "ln_eps", "ln_sqrt", "ln_rec", "ln_out", "x1_t", "x1_c", "y", "y_c", "y_tab",
                "y_1", "y_rest1", "y_2", "y_3", "y_parts")
FINISH_STEPS = ("both", "cnt", "cmax", "rcnt", "n2", "n2m", "n3", "n1_t", "n1_c", "n3_t", "n3_c", "emb",
                "b1cnt", "acc2", "srcy", "selfy", "sum", "relu", "relu_t", "relu_c", "n2_t", "n2_c", "out1",
                "o1", "x1_t", "x1_c", "out2", "bias", "o2", "res", "ln_sum", "ln_mean", "ln_cen", "ln_sq", "ln_var",
                "ln_eps", "ln_sqrt", "ln_rec", "ln_out")


def update_nodes(nc, sb, sem, bank, wt, bb, ident, table, y_tab, src_y, acc1_dram, x_rows, x_t, x1_dram, y_dram):
    with ExitStack() as cn:
        acc = sb("u_acc", [P, KB, WH], c=cn)
        xr = sb("u_xr", [P, KB, D], c=cn)
        xt = sb("u_xt", [D, KB * P], c=cn)
        yp = sb("u_yp", [P, KB, PARTS, D], BF16, c=cn)
        a, b, cen, sq, res = (sb(f"u_{n}", [P, KB, D], c=cn) for n in ("a", "b", "cen", "sq", "x1"))
        t1, t2 = (sb(f"u_{n}", [D, KB * P], c=cn) for n in ("t1", "t2"))
        sc = sb("u_sc", [P, 8, KB], c=cn)
        ps = bank[0][:, 0:KB * D].rearrange("p (k d) -> p k d", d=D)
        loaded, stored = sem("u_loaded"), sem("u_stored")
        turns = Turns(sem("u_step"), sem("u_pass"), UPDATE_STEPS)
        block = cn.enter_context(nc.Block())

        def broad(n):
            return bb[:, n:n + 1, :].to_broadcast([P, KB, D])

        def per_node(n):
            return sc[:, n, :].unsqueeze(2).to_broadcast([P, KB, D])

        @block.sync
        def _(sp):
            sp.sem_inc(turns.sem, 1)
            with sp.Fori(0, NB // KB) as e:
                sp.dma_start(acc[:, :, :], node_rows(acc1_dram, e)).then_inc(loaded, 16)
                sp.dma_start(xr[:, :, :], node_rows(x_rows, e)).then_inc(loaded, 16)
                sp.dma_start(xt[:, :], x_t[:, bass.ds(e * (KB * P), KB * P)]).then_inc(loaded, 16)
                turns.wait_all(sp, e)
                sp.dma_start(node_rows(x1_dram, e), res[:, :, :]).then_inc(stored, 16)
                sp.dma_start(node_rows(y_dram, e), yp[:, :, :, :].rearrange("p k a d -> p k (a d)")).then_inc(stored, 16)
                sp.wait_ge(stored, e * 32 + 32)
                sp.sem_inc(turns.passed, 1)

        @block.tensor
        def _(pe):
            with pe.Fori(0, NB // KB) as e:
                def step(name, ins):
                    ins().then_inc(turns.sem, 1)

                pe.wait_ge(loaded, e * 48 + 48)
                turns.wait_before(pe, e, "sumh_t")
                transpose_blocks(pe, bank, lambda k: acc[:, k, 0:D], ident).then_inc(turns.sem, 1)
                turns.wait_before(pe, e, "msg")
                multiply_blocks(pe, bank, [(t1, wt(W2M))]).then_inc(turns.sem, 1)
                turns.wait_before(pe, e, "mean_t")
                transpose_blocks(pe, bank, lambda k: a[:, k, :], ident).then_inc(turns.sem, 1)
                turns.wait_before(pe, e, "upd1")
                multiply_blocks(pe, bank, [(xt, wt(U1A)), (t2, wt(U1B))]).then_inc(turns.sem, 1)
                turns.wait_before(pe, e, "hu_t")
                transpose_blocks(pe, bank, lambda k: b[:, k, :], ident).then_inc(turns.sem, 1)
                turns.wait_before(pe, e, "upd2")
                multiply_blocks(pe, bank, [(t1, wt(W2U))]).then_inc(turns.sem, 1)
                turns.wait_before(pe, e, "x1_t")
                transpose_blocks(pe, bank, lambda k: res[:, k, :], ident).then_inc(turns.sem, 1)
                turns.wait_before(pe, e, "y")
                multiply_blocks(pe, bank, [(t1, wt(V1A))]).then_inc(turns.sem, 1)

        @block.scalar
        def _(act):
            with act.Fori(0, NB // KB) as e:
                turns.wait_before(act, e, "silu")
                act.activation(b[:, :, :], a[:, :, :], ACT.Silu).then_inc(turns.sem, 1)
                turns.wait_before(act, e, "ln_sqrt")
                act.activation(sc[:, 4, :], sc[:, 3, :], ACT.Sqrt).then_inc(turns.sem, 1)

        @block.vector
        def _(dve):
            with dve.Fori(0, NB // KB) as e:
                def before(name):
                    turns.wait_before(dve, e, name)

                before("sumh_c")
                copy_blocks(dve, bank, t1).then_inc(turns.sem, 1)
                before("cnt")
                dve.tensor_scalar(sc[:, 0, :], acc[:, :, D], 1e-6, None, ALU.add).then_inc(turns.sem, 1)
                before("rcnt")
                dve.reciprocal(sc[:, 1, :], sc[:, 0, :]).then_inc(turns.sem, 1)
                before("b2cnt")
                dve.tensor_tensor(a[:, :, :], broad(B2M), acc[:, :, D:G0].to_broadcast([P, KB, D]),
                                  ALU.mult).then_inc(turns.sem, 1)
                before("num")
                dve.tensor_tensor(a[:, :, :], a[:, :, :], ps, ALU.add).then_inc(turns.sem, 1)
                before("mean")
                dve.tensor_tensor(a[:, :, :], a[:, :, :], per_node(1), ALU.mult).then_inc(turns.sem, 1)
                before("mean_c")
                copy_blocks(dve, bank, t2).then_inc(turns.sem, 1)
                before("pre")
                dve.tensor_tensor(a[:, :, :], ps, broad(B1U), ALU.add).then_inc(turns.sem, 1)
                before("hu_c")
                copy_blocks(dve, bank, t1).then_inc(turns.sem, 1)
                before("new")
                dve.tensor_tensor(b[:, :, :], ps, broad(B2U), ALU.add).then_inc(turns.sem, 1)
                before("res")
                dve.tensor_tensor(b[:, :, :], b[:, :, :], xr[:, :, :], ALU.add).then_inc(turns.sem, 1)
                layernorm_steps(dve, before, turns, b, cen, sq, sc, per_node, res)
                before("x1_c")
                copy_blocks(dve, bank, t1).then_inc(turns.sem, 1)
                before("y_c")
                dve.tensor_copy(a[:, :, :], ps).then_inc(turns.sem, 1)
                before("y_tab")
                dve.tensor_tensor(src_y[:, bass.ds(e * KB, KB), :], a[:, :, :], a[:, :, :], ALU.subtract)
                dve.tensor_scalar(y_tab[:, bass.ds(e * KB, KB), :], a[:, :, :], 1.0, None, ALU.mult)\
                    .then_inc(turns.sem, 1)
                before("y_1")
                dve.tensor_copy(yp[:, :, 0, :], a[:, :, :]).then_inc(turns.sem, 1)
                before("y_rest1")
                dve.tensor_tensor(a[:, :, :], a[:, :, :], yp[:, :, 0, :], ALU.subtract).then_inc(turns.sem, 1)
                before("y_2")
                dve.tensor_copy(yp[:, :, 1, :], a[:, :, :]).then_inc(turns.sem, 1)
                before("y_3")
                dve.tensor_tensor(yp[:, :, 2, :], a[:, :, :], yp[:, :, 1, :], ALU.subtract).then_inc(turns.sem, 1)
                before("y_parts")
                dve.tensor_scalar(table[:, bass.ds(e * KB, KB), :, :].rearrange("p k a d -> p k (a d)"),
                                  yp[:, :, :, :].rearrange("p k a d -> p k (a d)"), 1.0, None, ALU.mult)\
                    .then_inc(turns.sem, 1)


def layernorm_steps(dve, before, turns, b, cen, sq, sc, per_node, res):
    before("ln_sum")
    dve.tensor_reduce(sc[:, 2, :], b[:, :, :], AX, ALU.add).then_inc(turns.sem, 1)
    before("ln_mean")
    dve.tensor_scalar(sc[:, 5, :], sc[:, 2, :], 1.0 / D, None, ALU.mult).then_inc(turns.sem, 1)
    before("ln_cen")
    dve.tensor_tensor(cen[:, :, :], b[:, :, :], per_node(5), ALU.subtract).then_inc(turns.sem, 1)
    before("ln_sq")
    dve.tensor_tensor(sq[:, :, :], cen[:, :, :], cen[:, :, :], ALU.mult).then_inc(turns.sem, 1)
    before("ln_var")
    dve.tensor_reduce(sc[:, 6, :], sq[:, :, :], AX, ALU.add).then_inc(turns.sem, 1)
    before("ln_eps")
    dve.tensor_scalar(sc[:, 3, :], sc[:, 6, :], 1.0 / D, 1e-5, ALU.mult, ALU.add).then_inc(turns.sem, 1)
    before("ln_rec")
    dve.reciprocal(sc[:, 7, :], sc[:, 4, :]).then_inc(turns.sem, 1)
    before("ln_out")
    dve.tensor_tensor(res[:, :, :], cen[:, :, :], per_node(7), ALU.mult).then_inc(turns.sem, 1)


def finish_nodes(nc, sb, sem, bank, wt, bb, ident, src_sum, y_tab, src_y, acc1_dram, acc2_dram, x1_dram, out):
    with ExitStack() as cn:
        acc = sb("f_acc", [P, KB, WH], c=cn)
        tot = sb("f_tot", [P, KB, W], c=cn)
        xr = sb("f_xr", [P, KB, D], c=cn)
        acc2 = sb("f_acc2", [P, KB, D], c=cn)
        a, b, cen, sq, res = (sb(f"f_{n}", [P, KB, D], c=cn) for n in ("a", "b", "cen", "sq", "res"))
        t1, t2 = (sb(f"f_{n}", [D, KB * P], c=cn) for n in ("t1", "t2"))
        sc = sb("f_sc", [P, 8, KB], c=cn)
        sd = sb("f_sd", [P, 2, KB], c=cn)
        ps = bank[0][:, 0:KB * D].rearrange("p (k d) -> p k d", d=D)
        loaded, stored = sem("f_loaded"), sem("f_stored")
        turns = Turns(sem("f_step"), sem("f_pass"), FINISH_STEPS)
        block = cn.enter_context(nc.Block())

        def broad(n):
            return bb[:, n:n + 1, :].to_broadcast([P, KB, D])

        def per_node(n):
            return sc[:, n, :].unsqueeze(2).to_broadcast([P, KB, D])

        @block.sync
        def _(sp):
            sp.sem_inc(turns.sem, 1)
            with sp.Fori(0, NB // KB) as e:
                sp.dma_start(acc[:, :, :], node_rows(acc1_dram, e)).then_inc(loaded, 16)
                sp.dma_start(acc2[:, :, :], node_rows(acc2_dram, e)).then_inc(loaded, 16)
                sp.dma_start(xr[:, :, :], node_rows(x1_dram, e)).then_inc(loaded, 16)
                turns.wait_all(sp, e)
                sp.dma_start(node_rows(out, e), res[:, :, :]).then_inc(stored, 16)
                sp.wait_ge(stored, e * 16 + 16)
                sp.sem_inc(turns.passed, 1)

        @block.tensor
        def _(pe):
            with pe.Fori(0, NB // KB) as e:
                turns.wait_before(pe, e, "n1_t")
                transpose_blocks(pe, bank, lambda k: tot[:, k, 0:D], ident).then_inc(turns.sem, 1)
                turns.wait_before(pe, e, "n3_t")
                transpose_blocks(pe, bank, lambda k: tot[:, k, 2 * D:3 * D], ident).then_inc(turns.sem, 1)
                turns.wait_before(pe, e, "emb")
                multiply_blocks(pe, bank, [(t1, wt(V1B)), (t2, wt(V1C))]).then_inc(turns.sem, 1)
                turns.wait_before(pe, e, "relu_t")
                transpose_blocks(pe, bank, lambda k: b[:, k, :], ident).then_inc(turns.sem, 1)
                turns.wait_before(pe, e, "n2_t")
                transpose_blocks(pe, bank, lambda k: tot[:, k, D:2 * D], ident).then_inc(turns.sem, 1)
                turns.wait_before(pe, e, "out1")
                multiply_blocks(pe, bank, [(t1, wt(Z2A)), (t2, wt(Z2C))]).then_inc(turns.sem, 1)
                turns.wait_before(pe, e, "x1_t")
                transpose_blocks(pe, bank, lambda k: xr[:, k, :], ident).then_inc(turns.sem, 1)
                turns.wait_before(pe, e, "out2")
                multiply_blocks(pe, bank, [(t1, wt(Z2B))]).then_inc(turns.sem, 1)

        @block.scalar
        def _(act):
            with act.Fori(0, NB // KB) as e:
                turns.wait_before(act, e, "ln_sqrt")
                act.activation(sc[:, 4, :], sc[:, 3, :], ACT.Sqrt).then_inc(turns.sem, 1)

        @block.vector
        def _(dve):
            with dve.Fori(0, NB // KB) as e:
                def before(name):
                    turns.wait_before(dve, e, name)

                def tt(name, o, x, y, op):
                    before(name)
                    dve.tensor_tensor(o, x, y, op).then_inc(turns.sem, 1)

                n2, n3 = tot[:, :, D:2 * D], tot[:, :, 2 * D:3 * D]
                dve.wait_ge(loaded, e * 48 + 48)
                tt("both", tot[:, :, :], acc[:, :, G0:WH], src_sum[:, bass.ds(e * KB, KB), :], ALU.add)
                before("cnt")
                dve.tensor_scalar(sc[:, 0, :], tot[:, :, W - 1], 1.0, None, ALU.add).then_inc(turns.sem, 1)
                before("cmax")
                dve.tensor_scalar(sd[:, 0, :], sc[:, 0, :], 1.0, None, ALU.max).then_inc(turns.sem, 1)
                before("rcnt")
                dve.reciprocal(sc[:, 1, :], sd[:, 0, :]).then_inc(turns.sem, 1)
                tt("n2", n2, n2, broad(TU), ALU.add)
                tt("n2m", n2, n2, per_node(1), ALU.mult)
                tt("n3", n3, n3, broad(TU), ALU.add)
                before("n1_c")
                copy_blocks(dve, bank, t1).then_inc(turns.sem, 1)
                before("n3_c")
                copy_blocks(dve, bank, t2).then_inc(turns.sem, 1)
                tt("b1cnt", a[:, :, :], broad(C1), per_node(0), ALU.mult)
                tt("acc2", a[:, :, :], a[:, :, :], acc2[:, :, :], ALU.add)
                tt("srcy", a[:, :, :], a[:, :, :], src_y[:, bass.ds(e * KB, KB), :], ALU.add)
                tt("selfy", a[:, :, :], a[:, :, :], y_tab[:, bass.ds(e * KB, KB), :], ALU.add)
                tt("sum", a[:, :, :], a[:, :, :], ps, ALU.add)
                before("relu")
                dve.tensor_scalar(b[:, :, :], a[:, :, :], 0.0, None, ALU.max).then_inc(turns.sem, 1)
                before("relu_c")
                copy_blocks(dve, bank, t1).then_inc(turns.sem, 1)
                before("n2_c")
                copy_blocks(dve, bank, t2).then_inc(turns.sem, 1)
                before("o1")
                dve.tensor_copy(a[:, :, :], ps).then_inc(turns.sem, 1)
                before("x1_c")
                copy_blocks(dve, bank, t1).then_inc(turns.sem, 1)
                tt("bias", b[:, :, :], ps, broad(C2), ALU.add)
                tt("o2", a[:, :, :], a[:, :, :], b[:, :, :], ALU.add)
                tt("res", b[:, :, :], a[:, :, :], xr[:, :, :], ALU.add)
                layernorm_steps(dve, before, turns, b, cen, sq, sc, per_node, res)


def sum_neighbours(nc, sb, sem, bank, iota_m, table, src_y, acc2_dram, y_dram, keys_dram, base_dram, ctl):
    RO2, RA = 4, 4
    with ExitStack() as c3:
        oh = sb("n_oh", [P, RO2, 2, CH, P], BF16, c=c3)
        adj = sb("n_adj", [P, RA, 4 * P], BF16, c=c3)
        keys = sb("n_keys", [P, 2, 2, NT], BF16, c=c3)
        yw = sb("n_yw", [P, 2, PARTS, D], BF16, c=c3)
        base = sb("n_base", [1, MAXSW * NL], I32, c=c3)
        dwin = sb("n_dwin", [P, 2, D], c=c3)
        unread = sb("n_unread", [P, 2, D3], BF16, c=c3)
        iob = sb("n_iob", [P, P], BF16, c=c3)
        adj_bank = [bank[0], bank[1], bank[2], bank[3]]
        srcb, dstb = [bank[4], bank[5]], bank[6]
        passed = sem("n_pass")
        consts = sem("n_consts")
        base_loaded = sem("n_base_loaded")
        keys_loaded = [Count(sem(f"n_keys_loaded{q}"), 16) for q in range(2)]
        yw_loaded = [Count(sem(f"n_yw_loaded{q}"), 16) for q in range(2)]
        oh_ready = Count(sem("n_oh_ready"), BC)
        adj_done = Count(sem("n_adj_done"), BC * NG)
        adj_copied = Count(sem("n_adj_copied"), BC * NG, credit=RA)
        adj_used = Count(sem("n_adj_used"), BC * (NG - 1), credit=RA)
        src_ready = Count(sem("n_src_ready"), BC, credit=BC)
        src_added = Count(sem("n_src_added"), BC, credit=4)
        dwin_saved = Count(sem("n_dwin_saved"), 2, credit=4)
        dwin_added = Count(sem("n_dwin_added"), 32, credit=32)
        block = c3.enter_context(nc.Block())

        def wait(eng, cnt, s, i, n):
            eng.wait_ge(cnt.sem, cnt.at(s, i, n))

        def hold(eng, cnt, s, i, n):
            wait(eng, cnt, s, i, n)
            eng.sem_inc(passed, 1)

        def sweep_count(eng, name):
            end = eng.alloc_register(name)
            eng.load(end, ctl[0:1, 1:2])
            return end

        @block.sync
        def _(sp):
            end = sweep_count(sp, "n_end_sp")
            for cnt in (adj_copied, adj_used, src_ready, src_added, dwin_saved):
                sp.sem_inc(cnt.sem, cnt.credit)
            with sp.Fori(0, end) as s:
                sp.dma_start(base[0:1, bass.ds(s * NL, NL)], base_dram[bass.ds(s, 1), :]).then_inc(base_loaded, 16)
                sp.wait_ge(base_loaded, s * 16 + 16)
                sp.sem_inc(passed, 1)
                with sp.Fori(0, BODIES) as i:
                    for q in range(2):
                        b = sp.value_load(base[0:1, bass.ds(s * NL + i * 2 + q, 1)], min_val=0, max_val=N - 1)
                        hold(sp, src_ready, s, i, NC_ * (q + 1) - BC)
                        sp.dma_start(yw[:, q, :, :].rearrange("p a d -> p (a d)"), y_dram[bass.ds(b, P), :]).then_inc(yw_loaded[q].sem, 16)
                        sp.dma_start(keys[:, q, :, :].rearrange("p a b -> p (a b)"),
                                     keys_dram[bass.ds((s * NL + i * 2 + q) * P, P), :])\
                            .then_inc(keys_loaded[q].sem, 16)

        @block.gpsimd
        def _(pool):
            end = sweep_count(pool, "n_end_pool")
            for r in range(2):
                pool.dma_start(unread[:, r, :], y_dram[0:P, :]).then_inc(dwin_added.sem, 16)
                pool.wait_ge(dwin_added.sem, 16 * (r + 1))
            with pool.Fori(0, end) as s:
                pool.wait_ge(base_loaded, s * 16 + 16)
                pool.sem_inc(passed, 1)
                with pool.Fori(0, BODIES) as i:
                    for q in range(2):
                        b = pool.value_load(base[0:1, bass.ds(s * NL + i * 2 + q, 1)], min_val=0, max_val=N - 1)
                        hold(pool, dwin_saved, s, i, q + 1)
                        hold(pool, dwin_added, s, i, 16 * q)
                        pool.dma_start(acc2_dram[bass.ds(b, P), :], dwin[:, q, :],
                                       accum_op=ALU.add).then_inc(dwin_added.sem, 16)
                hold(pool, dwin_added, s, BODIES, 0)

        @block.scalar
        def _(act):
            end = sweep_count(act, "n_end_act")
            with act.Fori(0, end) as s:
                with act.Fori(0, BODIES) as i:
                    for c in range(BC):
                        for g, (k0, kn) in enumerate(GROUPS):
                            n = c * NG + g
                            before, (cu, gu) = (n < RA), divmod((n - RA) % (BC * NG), NG)
                            if gu == NG - 1:
                                wait(act, src_ready, s, i, cu + 1 - before * BC)
                            else:
                                wait(act, adj_used, s, i, (cu - before * BC) * (NG - 1) + gu + 1)
                            wait(act, adj_done, s, i, n + 1)
                            act.activation(adj[:, n % RA, 0:2 * kn * P], adj_bank[n % 4][:, 0:2 * kn * P], ACT.Copy)\
                                .then_inc(adj_copied.sem, 1)
                act.sem_inc(passed, 1)

        @block.tensor
        def _(pe):
            end = sweep_count(pe, "n_end_pe")
            with pe.Fori(0, end) as s:
                with pe.Fori(0, BODIES) as i:
                    def adjacency(n):
                        c, g = n // NG, n % NG
                        k0, kn = GROUPS[g]
                        if g == 0:
                            wait(pe, oh_ready, s, i, c + 1)
                        wait(pe, adj_copied, s, i, n + 1 - 4)
                        for k in range(kn):
                            snd, rcv = oh[:, c % RO2, 0, k0 + k, :], oh[:, c % RO2, 1, k0 + k, :]
                            for m, (x, y) in enumerate(((snd, rcv), (rcv, snd))):
                                last = pe.matmul(adj_bank[n % 4][:, (2 * k + m) * P:(2 * k + m + 1) * P], x, y,
                                                 start=True, stop=True)
                        last.then_inc(adj_done.sem, 1)

                    def sums(n):
                        c, g = n // NG, n % NG
                        q, cc = c // NC_, c % NC_
                        k0, kn = GROUPS[g]
                        if g == 0:
                            wait(pe, src_added, s, i, c - 1)
                        if g == 0 and cc == 0:
                            wait(pe, yw_loaded[q], s, i, 16)
                            wait(pe, dwin_saved, s, i, q)
                        wait(pe, adj_copied, s, i, n + 1)
                        for k in range(kn):
                            t = k0 + k
                            b = cc * CH + t
                            to_rcv, to_snd = adj[:, n % RA, 2 * k * P:(2 * k + 1) * P], \
                                adj[:, n % RA, (2 * k + 1) * P:(2 * k + 2) * P]
                            for a in range(PARTS):
                                y = yw[:, q, a, :] if b == SELF else table[:, b, a, :]
                                pe.matmul(dstb[:, 0:D], to_rcv, y, start=(b == 0 and a == 0), stop=False)
                            for a in range(PARTS):
                                if b == SELF:
                                    last = pe.matmul(dstb[:, 0:D], to_snd, yw[:, q, a, :],
                                                     start=False, stop=(a == PARTS - 1))
                                else:
                                    last = pe.matmul(srcb[c % 2][:, t * D:(t + 1) * D], to_snd, yw[:, q, a, :],
                                                     start=(a == 0), stop=(a == PARTS - 1))
                        if g < NG - 1:
                            last.then_inc(adj_used.sem, 1)
                        if g == NG - 1:
                            last.then_inc(src_ready.sem, 1)

                    for n in range(BC * NG + 2):
                        if n < BC * NG:
                            adjacency(n)
                        if n >= 2:
                            sums(n - 2)
                pe.sem_inc(passed, 1)

        @block.vector
        def _(dve):
            end = sweep_count(dve, "n_end_dve")
            dve.tensor_copy(iob[:, :], iota_m[:, :]).then_inc(consts, 1)
            dve.wait_ge(consts, 1)
            with dve.Fori(0, end) as s:
                with dve.Fori(0, BODIES) as i:
                    def onehots(c):
                        q, b0 = c // NC_, c % NC_ * CH
                        if c % NC_ == 0:
                            wait(dve, keys_loaded[q], s, i, 16)
                        wait(dve, src_ready, s, i, c + 1 - RO2)
                        for m in range(2):
                            last = dve.tensor_tensor(oh[:, c % RO2, m, :, :],
                                                     keys[:, q, m, b0:b0 + CH].unsqueeze(2).to_broadcast([P, CH, P]),
                                                     iob[:, :].unsqueeze(1).to_broadcast([P, CH, P]), ALU.is_equal)
                        last.then_inc(oh_ready.sem, 1)

                    onehots(0)
                    onehots(1)
                    for c in range(BC):
                        q, b0 = c // NC_, c % NC_ * CH
                        if c + 2 < BC:
                            onehots(c + 2)
                        wait(dve, src_ready, s, i, c + 1)
                        kn = min(CH, NB - b0)
                        dve.tensor_tensor(src_y[:, b0:b0 + kn, :], src_y[:, b0:b0 + kn, :],
                                          srcb[c % 2][:, 0:kn * D].rearrange("p (k d) -> p k d", d=D),
                                          ALU.add).then_inc(src_added.sem, 1)
                        if c % NC_ == NC_ - 1:
                            hold(dve, dwin_added, s, i, 16 * q - 16)
                            dve.tensor_copy(dwin[:, q, :], dstb[:, 0:D]).then_inc(dwin_saved.sem, 1)
                dve.sem_inc(passed, 1)


def kernel(**inputs):
    import concourse.bacc as _bacc
    from concourse.bass_utils import run_bass_kernel_spmd as _run

    inp = {k: np.asarray(v) for k, v in inputs.items()}
    pad = NLX * LOT - E
    src = np.concatenate([inp["src"], np.full(pad, NB * P, inp["src"].dtype)])
    dst = np.pad(inp["dst"], (0, pad), mode="edge")

    def lots(v):
        return np.ascontiguousarray(v.reshape(NLX, P, T).transpose(1, 0, 2).reshape(P, NLX * T))

    x = np.concatenate([inp["x"], np.zeros((NROWS - N, D), inp["x"].dtype)])
    wm, wu, v1, z2 = inp["L0_gnn_W1_msg"], inp["L0_gnn_W1_upd"], inp["L1_gnn_W1"], inp["L1_gnn_W2"]
    blocks = [wm[0:D], wm[D:2 * D], wm[2 * D:], inp["L0_gnn_W2_msg"], wu[0:D], wu[D:], inp["L0_gnn_W2_upd"],
              v1[:, 0:D].T, v1[:, D:2 * D].T, v1[:, 2 * D:].T, z2[:, 0:D].T, z2[:, D:2 * D].T, z2[:, 2 * D:].T]
    rows = [inp["L0_gnn_b1_msg"], inp["L0_gnn_b2_msg"], inp["L0_gnn_b1_upd"], inp["L0_gnn_b2_upd"],
            inp["L1_gnn_b1"], inp["L1_gnn_b2"], inp["edge_attr_64_n2"][0]]
    arrays = {
        "edges": np.ascontiguousarray(np.concatenate(
            [inp["edge_attr_64"], inp["edge_attr_64_n2"], inp["edge_attr_64_n3"]], axis=1)),
        "src_t": lots(src), "dst_t": lots(dst), "x_t": np.ascontiguousarray(x.T), "x_rows": x,
        "wts": np.ascontiguousarray(np.concatenate(blocks, axis=1)),
        "bias": np.ascontiguousarray(np.concatenate(rows)[None]),
    }
    nc = _bacc.Bacc("TRN2", target_bir_lowering=False, num_devices=1)
    args = [nc.dram_tensor(k, a.shape, mybir.dt.from_np(a.dtype), kind="ExternalInput").ap() for k, a in arrays.items()]
    out = nc.dram_tensor("out", (NB * P, D), F32, kind="ExternalOutput").ap()
    gnn_kernel(nc, *args, out)
    r = _run(nc, [arrays], core_ids=[0])
    return r.results[0]["out"][:N]
```

```python
from contextlib import ExitStack

import numpy as np

import concourse.bass as bass
from concourse import mybir

F32 = mybir.dt.float32
BF16 = mybir.dt.bfloat16
F32R = mybir.dt.float32r
I32 = mybir.dt.int32
ALU = mybir.AluOpType
ACT = mybir.ActivationFunctionType
AX = mybir.AxisListType.X

P = 128
N = 6250
E = 206250
D = 64
NB = -(-N // P)
NROWS = (NB + 1) * P
T = 30
LOT = P * T
NL = -(-E // LOT)
NLX = NL + 2
NT = NB + 1
SELF = NB
CH = 5
KB = 7
NC_ = NT // CH
BC = 2 * NC_
BODIES = NL // 2
W = 3 * D + 2
G0 = D + 2
WH = G0 + W
GROUPS = ((0, 2), (2, 2), (4, 1))
NG = len(GROUPS)
SUMMED = [(c, g) for c in range(BC) for g in range(NG) if (c % NC_, g) != (NC_ - 1, NG - 1)]
MAXSW = NB + T + 1
RG = 5
RO = 3
RT = 4
LAG = CH + 2
SRC_LAG = 3
FAR = 8192.0
assert WH % 2 == 0 and W % 2 == 0 and RG <= BC and NT % CH == 0 and NB % KB == 0 and NL % 2 == 0 and BC * CH % RT == 0 and NT % 2 == 0

PARTS = 3
D3 = PARTS * D

WA, WB, WC, W2M, U1A, U1B, W2U, V1A, V1B, V1C, Z2A, Z2B, Z2C = range(13)
B1M, B2M, B1U, B2U, C1, C2, TU = range(7)


def previous_user(c, ring):
    if c >= ring:
        return c - ring
    last = [u for u in range(BC) if u % ring == c % ring][-1]
    return last - BC


def slot_uses(c, ring):
    uses = [u for u in range(BC) if u % ring == c % ring]
    return uses.index(c) + 1, len(uses)


class Count:

    def __init__(self, sem, body, extra=0, credit=0, sweep_bodies=BODIES):
        self.sem, self.body, self.credit = sem, body, credit
        self.sweep = body * sweep_bodies + extra

    def at(self, s, i, n):
        return s * self.sweep + i * self.body + (n + self.credit)


def gnn_kernel(nc, edges, src_t, dst_t, x_t, x_rows, wts, bias, out):
    ctx = ExitStack()
    with ctx:
        def sb(name, shape, dt=F32, c=ctx):
            return c.enter_context(nc.sbuf_tensor(name, shape, dt))

        def sem(name):
            return ctx.enter_context(nc.semaphore(name))

        xd_dram = nc.dram_tensor("xd_dram", (NROWS, 2 * D3), BF16, kind="Internal").ap()
        acc1_dram = nc.dram_tensor("acc1_dram", (NROWS, WH), F32, kind="Internal").ap()
        acc2_dram = nc.dram_tensor("acc2_dram", (NROWS, D), F32, kind="Internal").ap()
        y_dram = nc.dram_tensor("y_dram", (NROWS, D3), BF16, kind="Internal").ap()
        x1_dram = nc.dram_tensor("x1_dram", (NB * P, D), F32, kind="Internal").ap()
        keys_dram = nc.dram_tensor("keys_dram", (MAXSW * NL * P, 2 * NT), BF16, kind="Internal").ap()
        base_dram = nc.dram_tensor("base_dram", (MAXSW, NL), I32, kind="Internal").ap()

        bank = [ctx.enter_context(nc.psum_tensor(f"bank{b}", [P, 512], F32)) for b in range(8)]

        w = sb("w", [D, 13 * D])
        bb = sb("bb", [P, 7, D])
        ident = sb("ident", [P, P])
        ones = sb("ones", [P, P])
        iota_m = sb("iota_m", [P, P])
        ident_r = sb("ident_r", [P, P], F32R)
        src_sum = sb("src_sum", [P, NB, W])
        table = sb("table", [P, NB, PARTS, D], BF16)
        ctl = sb("ctl", [1, 4], I32)

        def wt(n):
            return w[:, n * D:(n + 1) * D]

        s_in = sem("s_in")
        s_c = sem("s_c")
        s_v0 = sem("s_v0")
        s_p0 = sem("s_p0")
        s_e0 = sem("s_e0")
        s_o0 = sem("s_o0")
        s_cv = sem("s_cv")
        s_xd = sem("s_xd")
        s_split = sem("s_split")

        sweep_ctx = ExitStack()
        hi = sb("hi", [P, NLX, T], BF16, c=sweep_ctx)
        dstf = sb("dstf", [P, NLX, T], c=sweep_ctx)
        rem = sb("rem", [P, NLX, T], BF16, c=sweep_ctx)
        lo1 = sb("lo1", [P, NLX, T], BF16, c=sweep_ctx)
        tri = sb("tri", [P, P], BF16, c=sweep_ctx)
        iota_b1 = sb("iota_b1", [P, NT], c=sweep_ctx)
        iota_p = sb("iota_p", [P, 1], c=sweep_ctx)
        iota_j = sb("iota_j", [P, T], BF16, c=sweep_ctx)
        lot0 = sb("lot0", [P, NLX], c=sweep_ctx)
        loops = sb("loops", [P, NLX, T], BF16, c=sweep_ctx)
        scanmask = sb("scanmask", [P, NT, T], BF16, c=sweep_ctx)

        with ExitStack() as c0:
            srci = sb("srci", [P, NLX * T], I32, c=c0)
            dsti = sb("dsti", [P, NLX * T], I32, c=c0)
            tmpi = sb("tmpi", [P, NLX * T], I32, c=c0)
            itmp = sb("itmp", [P, P], I32, c=c0)
            ibt = sb("ibt", [P, NT], I32, c=c0)
            ipt = sb("ipt", [P, 1], I32, c=c0)
            ijt = sb("ijt", [P, T], I32, c=c0)
            ilt = sb("ilt", [P, NLX], I32, c=c0)
            xt = sb("xt", [D, NROWS], c=c0)
            xdb = sb("xdb", [P, NB + 1, 2, D], c=c0)
            xparts = sb("xparts", [P, NB + 1, 2, PARTS, D], BF16, c=c0)
            other = sb("other", [P, NLX * T], c=c0)
            zero = src_sum[:, :, :].rearrange("p b f -> p (b f)")
            sender = xdb[:, :, :, :].rearrange("p b m d -> p (b m d)")[:, 0:NLX * T]
            block = c0.enter_context(nc.Block())
            NE0 = (NB + 1) // CH
            SH = 7
            assert P == 1 << SH

            @block.sync
            def _(sp):
                sp.dma_start(srci[:, :], src_t).then_inc(s_in, 16)
                sp.dma_start(dsti[:, :], dst_t).then_inc(s_in, 16)
                sp.dma_start(xt[:, :], x_t).then_inc(s_in, 16)
                sp.dma_start(w[:, :], wts).then_inc(s_in, 16)
                sp.dma_start(bb[:, :, :].rearrange("p a d -> p (a d)"),
                             bias.to_broadcast([P, 7 * D])).then_inc(s_in, 16)
                sp.wait_ge(s_c, 1)
                a1 = acc1_dram.rearrange("(p r) c -> p (r c)", p=P)
                for q in range(5):
                    sp.dma_start(a1[:, q * 10 * WH:(q + 1) * 10 * WH], zero[:, 0:10 * WH]).then_inc(s_o0, 16)
                a2 = acc2_dram.rearrange("(p r) c -> p (r c)", p=P)
                yz = y_dram.rearrange("(p r) c -> p (r c)", p=P)
                ky = (NB + 1) * D3 // 2
                for q in range(2):
                    k = (NB + 1) * D // 2
                    sp.dma_start(a2[:, q * k:(q + 1) * k], zero[:, 0:k]).then_inc(s_o0, 16)
                    sp.dma_start(yz[:, q * ky:(q + 1) * ky], zero[:, 0:ky // 2].bitcast(BF16)).then_inc(s_o0, 16)
                sp.wait_ge(s_split, 2)
                sp.dma_start(xd_dram.rearrange("(b p) d -> p b d", p=P),
                             xparts[:, :, :, :, :].rearrange("p b m a d -> p b (m a d)")).then_inc(s_xd, 16)
                sp.wait_ge(s_o0, 16 * 9)
                sp.wait_ge(s_xd, 16)

            @block.gpsimd
            def _(pool):
                pool.memset(src_sum[:, :, :], 0.0).then_inc(s_c, 1)
                pool.memset(ident[:, :], 0.0).then_inc(s_c, 1)
                pool.memset(ones[:, :], 1.0).then_inc(s_c, 1)
                pool.memset(tri[:, :], 1.0).then_inc(s_c, 1)
                pool.memset(scanmask[:, :, :], 1.0).then_inc(s_c, 1)
                pool.wait_ge(s_c, 5)
                pool.affine_select(out=ident[:, :], in_=ident[:, :], compare_op=ALU.not_equal, fill=1.0,
                                   base=0, pattern=[[-1, P]], channel_multiplier=1).then_inc(s_c, 1)
                pool.affine_select(out=tri[:, :], in_=tri[:, :], compare_op=ALU.is_gt, fill=0.0,
                                   base=0, pattern=[[1, P]], channel_multiplier=-1).then_inc(s_c, 1)
                pool.memset(scanmask[:, :, 0:1], 0.0).then_inc(s_c, 1)
                pool.iota(itmp[:, :], pattern=[[1, P]], base=0, channel_multiplier=0).then_inc(s_c, 1)
                pool.iota(ibt[:, :], pattern=[[1, NT]], base=1, channel_multiplier=0).then_inc(s_c, 1)
                pool.iota(ipt[:, :], pattern=[[1, 1]], base=0, channel_multiplier=1).then_inc(s_c, 1)
                pool.iota(ijt[:, :], pattern=[[1, T]], base=0, channel_multiplier=0).then_inc(s_c, 1)
                pool.iota(ilt[:, :], pattern=[[LOT, NLX]], base=0, channel_multiplier=0).then_inc(s_c, 1)
                pool.wait_ge(s_c, 13)
                pool.tensor_copy(iota_m[:, :], itmp[:, :]).then_inc(s_cv, 1)
                pool.tensor_copy(iota_b1[:, :], ibt[:, :]).then_inc(s_cv, 1)
                pool.tensor_copy(iota_p[:, :], ipt[:, :]).then_inc(s_cv, 1)
                pool.tensor_copy(iota_j[:, :], ijt[:, :]).then_inc(s_cv, 1)
                pool.tensor_copy(lot0[:, :], ilt[:, :]).then_inc(s_cv, 1)
                pool.wait_ge(s_cv, 5)

            @block.tensor
            def _(pe):
                pe.wait_ge(s_in, 80)
                for e in range(NE0):
                    if e >= 2:
                        pe.wait_ge(s_e0, e - 1)
                    for k in range(CH):
                        b = e * CH + k
                        lhs = xt[:, b * P:(b + 1) * P]
                        pe.matmul(bank[e % 2][:, k * D:(k + 1) * D], lhs, wt(WB), start=True, stop=True)
                        last = pe.matmul(bank[2 + e % 2][:, k * D:(k + 1) * D], lhs, wt(WC), start=True, stop=True)
                    last.then_inc(s_p0, 1)

            @block.vector
            def _(dve):
                done = [0]

                def step(ins):
                    ins.then_inc(s_v0, 1)
                    done[0] += 1
                    dve.wait_ge(s_v0, done[0])

                for e in range(NE0):
                    dve.wait_ge(s_p0, e + 1)
                    b0 = e * CH
                    nd = CH
                    snd = bank[e % 2][:, 0:nd * D].rearrange("p (k d) -> p k d", d=D)
                    dve.tensor_copy(xdb[:, b0:b0 + nd, 1, :], snd)
                    dve.tensor_tensor(xdb[:, b0:b0 + nd, 0, :],
                                      bank[2 + e % 2][:, 0:nd * D].rearrange("p (k d) -> p k d", d=D),
                                      bb[:, B1M:B1M + 1, :].to_broadcast([P, nd, D]), ALU.add).then_inc(s_e0, 1)
                dve.wait_ge(s_e0, NE0)
                for a in range(PARTS):
                    step(dve.tensor_copy(xparts[:, :, :, a, :], xdb[:, :, :, :]))
                    if a < PARTS - 1:
                        step(dve.tensor_tensor(xdb[:, :, :, :], xdb[:, :, :, :], xparts[:, :, :, a, :], ALU.subtract))
                dve.sem_inc(s_split, 2)
                step(dve.tensor_copy(table[:, :, :, :].rearrange("p b a d -> p b (a d)"),
                                     xparts[:, 0:NB, 1, :, :].rearrange("p b a d -> p b (a d)")))
                f = "p l t -> p (l t)"
                def flat(v):
                    return v[:, :, :].rearrange(f)

                step(dve.tensor_copy(sender, srci[:, :]))
                step(dve.tensor_scalar(flat(rem), sender, float(NB * P) - 0.5, None, ALU.is_lt))
                step(dve.tensor_copy(flat(dstf), dsti[:, :]))
                step(dve.tensor_tensor(flat(loops), sender, flat(dstf), ALU.is_equal))
                step(dve.tensor_tensor(other[:, :], sender, flat(dstf), ALU.not_equal))
                step(dve.tensor_scalar(tmpi[:, :], srci[:, :], SH, None, ALU.arith_shift_right))
                step(dve.tensor_scalar(dsti[:, :], srci[:, :], P - 1, None, ALU.bitwise_and))
                step(dve.tensor_copy(sender, tmpi[:, :]))
                step(dve.scalar_tensor_tensor(sender, sender, -float(SELF), other[:, :], ALU.add, ALU.mult))
                step(dve.tensor_scalar(flat(hi), sender, float(SELF), None, ALU.add))
                step(dve.scalar_tensor_tensor(flat(lo1), dsti[:, :], 1.0, other[:, :], ALU.add, ALU.mult))
                step(dve.memset(ctl[:, :], 0))

        gh_ready = [sem(f"gh_ready{r}") for r in range(RG)]
        gh_use = {}
        for c in range(BC):
            gh_use[c] = slot_uses(c, RG)
        gh_count = [Count(gh_ready[r], 16 * CH * len([c for c in range(BC) if c % RG == r])) for r in range(RG)]
        idx_ready = Count(sem("idx_ready"), 2, extra=2, credit=4)
        oh_ready = Count(sem("oh_ready"), BC)
        copied = Count(sem("copied"), BC * CH, credit=4)
        h_ready = Count(sem("h_ready"), BC, credit=4)
        h_raw = Count(sem("h_raw"), BC, credit=4)
        hhi_ready = Count(sem("hhi_ready"), BC, credit=4)
        hi_ready = Count(sem("hi_ready"), BC, credit=4)
        lo_ready = Count(sem("lo_ready"), BC, credit=BC)
        trans = Count(sem("trans"), BC * CH, credit=BC * CH)
        pre_done = Count(sem("pre_done"), BC, credit=BC)
        srcsum_ready = Count(sem("srcsum_ready"), len(SUMMED))
        srcsum_added = Count(sem("srcsum_added"), len(SUMMED), credit=4)
        dst_summed = Count(sem("dst_summed"), BC, credit=BC)
        dwin_saved = Count(sem("dwin_saved"), 2, extra=1, credit=4)
        dwin_added = Count(sem("dwin_added"), 32, extra=16, credit=16)
        xdw_ready = [Count(sem(f"xdw_ready{q}"), 16) for q in range(2)]
        keys_saved = [Count(sem(f"keys_saved{q}"), 16, credit=32) for q in range(2)]
        count_ready = Count(sem("count_ready"), 2, extra=2)
        prefix_done = Count(sem("prefix_done"), 2, extra=2)
        spread_ready = Count(sem("spread_ready"), 2, extra=2)
        inverted = Count(sem("inverted"), 2, extra=2)
        base_min = Count(sem("base_min"), 0, extra=1)
        base_t = Count(sem("base_t"), 0, extra=1)
        base_col = Count(sem("base_col"), 0, extra=1)
        base_bc = Count(sem("base_bc"), 0, extra=1)
        base_set = Count(sem("base_set"), 0, extra=1)
        base_saved = Count(sem("base_saved"), 0, extra=16, credit=16)
        left_ready = Count(sem("left_ready"), 0, extra=1)
        left_total = Count(sem("left_total"), 0, extra=1)
        sweep_end = Count(sem("sweep_end"), 0, extra=1)
        s_pass = sem("s_pass")
        s_chain = sem("s_chain")

        def wait(eng, cnt, s, i, n):
            eng.wait_ge(cnt.sem, cnt.at(s, i, n))

        def hold(eng, cnt, s, i, n):
            eng.wait_ge(cnt.sem, cnt.at(s, i, n))
            eng.sem_inc(s_pass, 1)

        with sweep_ctx, ExitStack() as c1:
            raw = sb("raw", [P, RG, CH, 3 * D], c=c1)
            hraw = sb("hraw", [P, 2, CH, D], c=c1)
            ghi = sb("ghi", [P, RO, CH, WH], F32R, c=c1)
            glo = sb("glo", [P, RO, CH, WH], F32R, c=c1)
            oh = sb("oh", [P, RO, 2, CH, P], F32R, c=c1)
            tcopy = sb("tcopy", [P, RT, 2 * P], BF16, c=c1)
            rcopy = sb("rcopy", [D, RT, P], c=c1)
            onehot_b = sb("onehot_b", [P, NT, T], BF16, c=c1)
            run = sb("run", [P, NT, T], c=c1)
            vals = sb("vals", [P, 4, NT, T], BF16, c=c1)
            slot_oh = sb("slot_oh", [P, T, P], BF16, c=c1)
            khi = sb("khi", [P, NLX, T], c=c1)
            dl1 = sb("dl1", [P, NLX, T], BF16, c=c1)
            scratch = vals[:, :, :, :].rearrange("p a b t -> p (a b t)")[:, 0:2 * NLX * T].bitcast(F32)\
                .rearrange("p (l t) -> p l t", t=T)
            inw = slot_oh[:, :, :].rearrange("p a b -> p (a b)")[:, 0:2 * NLX * T].bitcast(F32)\
                .rearrange("p (l t) -> p l t", t=T)
            hist = sb("hist", [P, NT], BF16, c=c1)
            rank = sb("rank", [P, T], c=c1)
            placed = sb("placed", [P, T], c=c1)
            invs = sb("invs", [P, 2, NT], c=c1)
            idf = sb("idf", [P, NT], c=c1)
            idx = sb("idx", [P, 2, NT], I32, c=c1)
            keys = sb("keys", [P, 2, 2, NT], BF16, c=c1)
            sl1 = sb("sl1", [P, NLX, T], BF16, c=c1)
            xdw = sb("xdw", [P, 2, 2, PARTS, D], BF16, c=c1)
            dwin = sb("dwin", [P, 2, WH], c=c1)
            unread = sb("unread", [P, 2 * D3], BF16, c=c1)
            minp = sb("minp", [P, NLX], c=c1)
            bcol = sb("bcol", [P, 2], c=c1)
            bdiag = sb("bdiag", [NLX, NLX], c=c1)
            base_f = sb("base_f", [P, NLX], c=c1)
            base_i = sb("base_i", [1, NLX + 1], I32, c=c1)
            left = sb("left", [P, 2], c=c1)
            swf = sb("swf", [1, 4], c=c1)
            tb, pb, db, rb, sbk = [bank[0], bank[1]], [bank[2], bank[3]], bank[4], bank[5], [bank[6], bank[7]]
            block = c1.enter_context(nc.Block())

            def sweeps(eng, name):
                end = eng.alloc_register(name)
                eng.reg_mov(end, 1)
                return end

            @block.sync
            def _(sp):
                end = sweeps(sp, "sweep_end_sp")
                for cnt in (idx_ready, copied, h_ready, h_raw, hhi_ready, hi_ready, lo_ready, trans, pre_done, srcsum_added, dst_summed, dwin_saved,
                            keys_saved[0], keys_saved[1], base_saved):
                    sp.sem_inc(cnt.sem, cnt.credit)
                with sp.Fori(0, end) as s:
                    sp.wait_ge(base_set.sem, base_set.at(s, 0, 1))
                    sp.dma_start(base_dram[bass.ds(s, 1), :], base_i[0:1, 1:1 + NL]).then_inc(base_saved.sem, 16)
                    with sp.Fori(0, BODIES) as i:
                        for q in range(2):
                            b = sp.value_load(base_i[0:1, bass.ds(i * 2 + (1 + q), 1)], min_val=0, max_val=N - 1)
                            hold(sp, pre_done, s, i, NC_ * (q + 1) - BC)
                            sp.dma_start(xdw[:, q, :, :, :].rearrange("p m a d -> p (m a d)"), xd_dram[bass.ds(b, P), :]).then_inc(xdw_ready[q].sem, 16)
                            hold(sp, idx_ready, s, i, q + 1)
                            sp.dma_start(keys_dram[bass.ds((s * NL + i * 2 + q) * P, P), :],
                                         keys[:, q, :, :].rearrange("p a b -> p (a b)")).then_inc(keys_saved[q].sem, 16)
                    hold(sp, sweep_end, s, 0, 1)
                    sp.load(end, ctl[0:1, 0:1])
                    hold(sp, base_saved, s, 0, 16)

            @block.gpsimd
            def _(pool):
                end = sweeps(pool, "sweep_end_pool")
                for part, one in ((ghi, 1.0), (glo, 0.0)):
                    for col in (D, WH - 2):
                        pool.memset(part[:, :, :, col:col + 1].bitcast(F32), one).then_inc(s_c, 1)
                        pool.memset(part[:, :, :, col + 1:col + 2].bitcast(F32), 0.0).then_inc(s_c, 1)
                pool.dma_start(unread[:, :], xd_dram[0:P, :]).then_inc(dwin_added.sem, 16)
                pool.wait_ge(s_c, 21)

                def add_window(s, i, q, n):
                    b = pool.value_load(base_i[0:1, bass.ds(i * 2 + q, 1)], min_val=0, max_val=N - 1)
                    hold(pool, dwin_saved, s, i, n + 1)
                    hold(pool, dwin_added, s, i, 16 * n)
                    pool.dma_start(acc1_dram[bass.ds(b, P), :], dwin[:, (q + 1) % 2, :],
                                   accum_op=ALU.add).then_inc(dwin_added.sem, 16)

                with pool.Fori(0, end) as s:
                    hold(pool, base_set, s, 0, 1)
                    with pool.Fori(0, BODIES) as i:
                        for c in range(BC):
                            if c % NC_ == 0:
                                hold(pool, idx_ready, s, i, c // NC_ + 1)
                            hold(pool, trans, s, i, (previous_user(c, RG) + 1) * CH)
                            hold(pool, lo_ready, s, i, previous_user(c, RG) + 1)
                            for k in range(CH):
                                t = c % NC_ * CH + k
                                pool.indirect_dma_start(
                                    out=raw[:, c % RG, k, :], out_offset=None, in_=edges,
                                    in_offset=bass.IndirectOffsetOnAxis(ap=idx[:, c // NC_, t:t + 1], axis=0),
                                ).then_inc(gh_ready[c % RG], 16)
                            if c == 6:
                                add_window(s, i, 0, 0)
                            if c == NC_ + 7:
                                add_window(s, i, 1, 1)
                    add_window(s, BODIES, 0, 0)
                    hold(pool, dwin_added, s, BODIES, 16)
                    hold(pool, sweep_end, s, 0, 1)
                    pool.load(end, ctl[0:1, 0:1])

            @block.scalar
            def _(act):
                end = sweeps(act, "sweep_end_act")

                def high_part(s, i, c):
                    act.wait_ge(gh_ready[c % RG], gh_count[c % RG].at(s, i, 16 * CH * gh_use[c][0]))
                    act.wait_ge(dst_summed.sem, dst_summed.at(s, i, previous_user(c, RO) + 1))
                    act.activation(ghi[:, c % RO, :, G0:G0 + 3 * D], raw[:, c % RG, :, :], ACT.Copy)\
                        .then_inc(hi_ready.sem, 1)

                def activations(s, i, c):
                    act.wait_ge(pre_done.sem, pre_done.at(s, i, c + 1))
                    act.wait_ge(h_ready.sem, h_ready.at(s, i, c - 1))
                    act.activation(hraw[:, c % 2, :, :], pb[c % 2][:, 0:CH * D].rearrange("p (k d) -> p k d", d=D),
                                   ACT.Silu).then_inc(h_raw.sem, 1)
                    act.wait_ge(h_raw.sem, h_raw.at(s, i, c + 1))
                    act.activation(ghi[:, c % RO, :, 0:D], hraw[:, c % 2, :, :], ACT.Copy).then_inc(hhi_ready.sem, 1)

                with act.Fori(0, end) as s:
                    with act.Fori(0, BODIES) as i:
                        for t in range(BC * CH):
                            c, k = t // CH, t % CH
                            if t == 0:
                                high_part(s, i, 0)
                            if k == 2 and c + 1 < BC:
                                high_part(s, i, c + 1)
                            act.wait_ge(trans.sem, trans.at(s, i, t + 1))
                            act.activation(tcopy[:, t % RT, :], tb[t % 2][:, 0:2 * P], ACT.Copy)
                            act.activation(rcopy[:, t % RT, :], tb[t % 2][0:D, 2 * P:3 * P], ACT.Copy)\
                                .then_inc(copied.sem, 1)
                            if k == 0 and c > 0:
                                activations(s, i, c - 1)
                            if t == BC * CH - 1:
                                activations(s, i, c)
                    hold(act, sweep_end, s, 0, 1)
                    act.load(end, ctl[0:1, 0:1])

            @block.tensor
            def _(pe):
                end = sweeps(pe, "sweep_end_pe")

                def prefix(s, i, n):
                    wait(pe, count_ready, s, i, n + 1)
                    pe.matmul(rb[:, 0:NT], tri[:, :], hist[:, :], start=True, stop=True).then_inc(prefix_done.sem, 1)

                def invert(s, i, n):
                    wait(pe, spread_ready, s, i, n + 1)
                    for j in range(T):
                        last = pe.matmul(rb[:, 64:64 + 4 * NT], slot_oh[:, j, :],
                                         vals[:, :, :, j].rearrange("p a b -> p (a b)"),
                                         start=(j == 0), stop=(j == T - 1))
                    last.then_inc(inverted.sem, 1)

                with pe.Fori(0, end) as s:
                    hold(pe, base_min, s, 0, 1)
                    pe.transpose(rb[0:NLX, 0:P], minp[:, :], ident[:, :]).then_inc(base_t.sem, 1)
                    wait(pe, base_col, s, 0, 1)
                    pe.matmul(rb[:, 0:NLX], ones[0:NLX, :], bdiag[:, :], start=True, stop=True)\
                        .then_inc(base_bc.sem, 1)
                    for q in range(2):
                        prefix(s, 0, q)
                        invert(s, 0, q)

                    with pe.Fori(0, BODIES) as i:
                        def products(t):
                            c, k = t // CH, t % CH
                            b = t % NT
                            o = pb[c % 2][:, k * D:(k + 1) * D]
                            if k == 0:
                                wait(pe, h_raw, s, i, c - 1)
                            if b == 0:
                                wait(pe, xdw_ready[c // NC_], s, i, 16)
                            wait(pe, copied, s, i, t + 1)
                            tc = tcopy[:, t % RT, :]
                            for a in range(PARTS):
                                senders = xdw[:, c // NC_, 1, a, :] if b == SELF else table[:, b, a, :]
                                pe.matmul(o, tc[:, 0:P], senders, start=(a == 0), stop=False)
                            for a in range(PARTS):
                                pe.matmul(o, tc[:, P:2 * P], xdw[:, c // NC_, 0, a, :], start=False, stop=False)
                            last = pe.matmul(o, rcopy[:, t % RT, :], wt(WA), start=False, stop=True)
                            if k == CH - 1:
                                last.then_inc(pre_done.sem, 1)

                        def dst_sum(t):
                            c, k = t // CH, t % CH
                            b = t % NT
                            if k == 0:
                                wait(pe, h_ready, s, i, c + 1)
                            if b == 0:
                                wait(pe, dwin_saved, s, i, c // NC_ + 1)
                            rcv = oh[:, c % RO, 1, k, :]
                            pe.matmul(db[:, 0:WH], rcv, ghi[:, c % RO, k, :], start=(b == 0), stop=False)
                            last = pe.matmul(db[:, 0:WH], rcv, glo[:, c % RO, k, :], start=False, stop=(b == NT - 1))
                            if b == SELF:
                                for part in (ghi, glo):
                                    last = pe.matmul(db[:, G0:WH], rcv, part[:, c % RO, k, G0:WH],
                                                     start=False, stop=True, skip_group_check=True)
                            if k == CH - 1:
                                last.then_inc(dst_summed.sem, 1)

                        def src_group_sum(t):
                            c, k = t // CH, t % CH
                            g = [n for n, (k0, kn) in enumerate(GROUPS) if k0 <= k < k0 + kn][0]
                            k0, kn = GROUPS[g]
                            n = SUMMED.index((c, g))
                            if k == k0:
                                wait(pe, srcsum_added, s, i, n - 1)
                            if k == 0:
                                wait(pe, lo_ready, s, i, c + 1)
                            for part in (ghi, glo):
                                last = pe.matmul(sbk[n % 2][:, (k - k0) * W:(k - k0 + 1) * W],
                                                 oh[:, c % RO, 0, k, :], part[:, c % RO, k, G0:WH],
                                                 start=(part is ghi), stop=(part is glo))
                            if k == k0 + kn - 1:
                                last.then_inc(srcsum_ready.sem, 1)

                        for t in range(BC * CH + LAG):
                            if t < BC * CH:
                                c, k = t // CH, t % CH
                                if k == 0:
                                    wait(pe, oh_ready, s, i, c + 1)
                                    wait(pe, gh_count[c % RG], s, i, 16 * CH * gh_use[c][0])
                                wait(pe, copied, s, i, t - 1)
                                for m in range(2):
                                    pe.transpose(tb[t % 2][:, m * P:(m + 1) * P].bitcast(F32R),
                                                 oh[:, c % RO, m, k, :], ident_r[:, :])
                                pe.transpose(tb[t % 2][0:D, 2 * P:3 * P], raw[:, c % RG, k, 0:D],
                                             ident[:, :]).then_inc(trans.sem, 1)
                            if SRC_LAG <= t < BC * CH + SRC_LAG and (t - SRC_LAG) % NT != SELF:
                                src_group_sum(t - SRC_LAG)
                            if 1 <= t <= BC * CH:
                                products(t - 1)
                            q, u = divmod(t, NT)
                            if q < 2 and u == 2 * CH + 3:
                                prefix(s, i, 2 + q)
                            if q < 2 and u == 9 * CH + 1:
                                invert(s, i, 2 + q)
                            if t >= LAG:
                                dst_sum(t - LAG)
                    wait(pe, left_ready, s, 0, 1)
                    pe.matmul(rb[:, 0:1], ones[:, :], left[:, 0:1], start=True, stop=True).then_inc(left_total.sem, 1)
                    hold(pe, sweep_end, s, 0, 1)
                    pe.load(end, ctl[0:1, 0:1])

            @block.vector
            def _(dve):
                end = sweeps(dve, "sweep_end_dve")
                links = {"pro": 0, "body": 0, "end": 0}
                plan = {"pro": LINKS_PRO, "body": LINKS_BODY, "end": LINKS_END}
                per_sweep = LINKS_PRO + LINKS_BODY * BODIES + LINKS_END

                def link(ins, part, s, i):
                    ins.then_inc(s_chain, 1)
                    links[part] += 1
                    n = links[part] + (plan["pro"] if part != "pro" else 0)
                    if part == "end":
                        n += plan["body"] * BODIES
                    dve.wait_ge(s_chain, s * per_sweep + i * plan["body"] + n)

                def deal_tiles(part, s, i, l):
                    link(dve.tensor_tensor(onehot_b[:, :, :],
                                           khi[:, bass.ds(l, 1), :].to_broadcast([P, NT, T]),
                                           iota_b1[:, :].unsqueeze(2).to_broadcast([P, NT, T]), ALU.is_equal),
                         part, s, i)

                def deal_counts():
                    with nc.allow_low_precision("counts of at most 30 are exact"):
                        dve.tensor_reduce(hist[:, :], onehot_b[:, :, :], AX, ALU.add).then_inc(count_ready.sem, 1)

                def deal_scan(part, s, i, n):
                    link(dve.tensor_copy(run[:, :, :], onehot_b[:, :, :]), part, s, i)
                    wait(dve, prefix_done, s, i, n + 1)
                    link(dve.tensor_tensor(run[:, :, 0:1], run[:, :, 0:1], rb[:, 0:NT].unsqueeze(2), ALU.add),
                         part, s, i)
                    flat = "p b t -> p (b t)"
                    link(dve.tensor_tensor_scan(run[:, :, :].rearrange(flat), scanmask[:, :, :].rearrange(flat),
                                                run[:, :, :].rearrange(flat), 0.0, ALU.mult, ALU.add), part, s, i)

                def deal_own_count(part, s, i):
                    link(dve.tensor_tensor(run[:, :, :], run[:, :, :], onehot_b[:, :, :], ALU.mult), part, s, i)

                def deal_ranks(part, s, i, l):
                    link(dve.tensor_reduce(rank[:, :], run[:, :, :].rearrange("p b t -> p t b"), AX, ALU.add),
                         part, s, i)
                    link(dve.tensor_scalar(placed[:, :], rank[:, :], float(P) + 0.5, None, ALU.is_lt), part, s, i)
                    link(dve.scalar_tensor_tensor(placed[:, :], rank[:, :], 0.5, placed[:, :], ALU.is_gt, ALU.mult),
                         part, s, i)
                    dve.tensor_tensor(rem[:, bass.ds(l, 1), :], rem[:, bass.ds(l, 1), :],
                                      placed[:, :].unsqueeze(1), ALU.subtract)
                    link(dve.tensor_scalar(rank[:, :], rank[:, :], -1.0, None, ALU.add), part, s, i)

                def deal_places(part, s, i, half):
                    j0, j1 = half * T // 2, (half + 1) * T // 2
                    link(dve.tensor_tensor(slot_oh[:, j0:j1, :], rank[:, j0:j1].unsqueeze(2).to_broadcast([P, j1 - j0, P]),
                                           iota_m[:, :].unsqueeze(1).to_broadcast([P, j1 - j0, P]), ALU.is_equal),
                         part, s, i)

                def deal_numbers():
                    dve.tensor_scalar(vals[:, 0, :, :], onehot_b[:, :, :], iota_p[:, 0:1], None, ALU.mult)
                    dve.tensor_tensor(vals[:, 1, :, :], onehot_b[:, :, :],
                                      iota_j[:, :].unsqueeze(1).to_broadcast([P, NT, T]), ALU.mult)

                def deal_senders(l):
                    dve.tensor_tensor(vals[:, 2, :, :], onehot_b[:, :, :],
                                      sl1[:, bass.ds(l, 1), :].to_broadcast([P, NT, T]), ALU.mult)

                def deal_receivers(l):
                    dve.tensor_tensor(vals[:, 3, :, :], onehot_b[:, :, :],
                                      dl1[:, bass.ds(l, 1), :].to_broadcast([P, NT, T]),
                                      ALU.mult).then_inc(spread_ready.sem, 1)

                def deal_keys(part, s, i, l, q, n):
                    wait(dve, inverted, s, i, n + 1)
                    wait(dve, keys_saved[q], s, i, 16 if n >= 2 else 0)
                    link(dve.tensor_copy(invs[:, :, :], rb[:, 64:64 + 2 * NT].rearrange("p (a b) -> p a b", a=2)),
                         part, s, i)
                    link(dve.scalar_tensor_tensor(idf[:, :], invs[:, 0, :], float(T), invs[:, 1, :],
                                                  ALU.mult, ALU.add), part, s, i)
                    dve.tensor_scalar(idx[:, q, :], idf[:, :], lot0[:, bass.ds(l, 1)], None, ALU.add)
                    link(dve.tensor_scalar(keys[:, q, :, :],
                                           rb[:, 64 + 2 * NT:64 + 4 * NT].rearrange("p (a b) -> p a b", a=2),
                                           -1.0, None, ALU.add), part, s, i)
                    dve.sem_inc(idx_ready.sem, 1)

                def onehots(s, i, c):
                    q, b0 = c // NC_, c % NC_ * CH
                    wait(dve, dst_summed, s, i, previous_user(c, RO) + 1)
                    for m in range(2):
                        last = dve.tensor_tensor(
                            oh[:, c % RO, m, :, :],
                            keys[:, q, m, b0:b0 + CH].unsqueeze(2).to_broadcast([P, CH, P]),
                            iota_m[:, :].unsqueeze(1).to_broadcast([P, CH, P]), ALU.is_equal)
                    last.then_inc(oh_ready.sem, 1)

                def low_part(s, i, c):
                    wait(dve, hi_ready, s, i, c + 1)
                    dve.tensor_tensor(glo[:, c % RO, :, G0:G0 + 3 * D], raw[:, c % RG, :, :],
                                      ghi[:, c % RO, :, G0:G0 + 3 * D].bitcast(F32),
                                      ALU.subtract).then_inc(lo_ready.sem, 1)

                def low_part_h(s, i, c):
                    wait(dve, hhi_ready, s, i, c + 1)
                    dve.tensor_tensor(glo[:, c % RO, :, 0:D], hraw[:, c % 2, :, :],
                                      ghi[:, c % RO, :, 0:D].bitcast(F32), ALU.subtract).then_inc(h_ready.sem, 1)

                def save_window(s, i, q):
                    wait(dve, dst_summed, s, i, NC_ * (q + 1))
                    wait(dve, dwin_added, s, i, 16 * q)
                    dve.tensor_copy(dwin[:, q, :], db[:, 0:WH]).then_inc(dwin_saved.sem, 1)

                def add_group(s, i, c, g):
                    k0, kn = GROUPS[g]
                    b0 = c % NC_ * CH + k0
                    n = SUMMED.index((c, g))
                    wait(dve, srcsum_ready, s, i, n + 1)
                    dve.tensor_tensor(src_sum[:, b0:b0 + kn, :], src_sum[:, b0:b0 + kn, :],
                                      sbk[n % 2][:, 0:kn * W].rearrange("p (k f) -> p k f", f=W),
                                      ALU.add).then_inc(srcsum_added.sem, 1)

                dve.tensor_copy(ident_r[:, :], ident[:, :]).then_inc(s_v0, 1)
                dve.memset(base_i[:, :], 0).then_inc(s_v0, 1)
                dve.memset(swf[:, :], 0.0).then_inc(s_v0, 1)
                dve.wait_ge(s_v0, 15 + 2 * PARTS)
                dve.wait_ge(s_c, 21)
                with dve.Fori(0, end) as s:
                    p0 = ("pro", s, 0)
                    link(dve.scalar_tensor_tensor(khi[:, :, :], dstf[:, :, :], -FAR, rem[:, :, :], ALU.add, ALU.mult), *p0)
                    dve.tensor_reduce(minp[:, :], khi[:, :, :], AX, ALU.min).then_inc(base_min.sem, 1)
                    wait(dve, base_t, s, 0, 1)
                    link(dve.tensor_reduce(bcol[0:NLX, 0:1], rb[0:NLX, 0:P], AX, ALU.min), *p0)
                    link(dve.tensor_scalar(bcol[0:NLX, 1:2], bcol[0:NLX, 0:1], FAR, float(N - 1), ALU.add, ALU.min), *p0)
                    link(dve.tensor_scalar(bdiag[:, :], ident[0:NLX, 0:NLX], bcol[0:NLX, 1:2], None, ALU.mult), *p0)
                    dve.sem_inc(base_col.sem, 1)
                    wait(dve, base_bc, s, 0, 1)
                    wait(dve, base_saved, s, 0, 0)
                    wait(dve, dwin_added, s, 0, 0)
                    dve.memset(dwin[:, 1, :], 0.0).then_inc(dwin_saved.sem, 1)
                    link(dve.tensor_copy(base_f[:, :], rb[:, 0:NLX]), *p0)
                    link(dve.tensor_copy(base_i[0:1, 1:1 + NLX], base_f[0:1, :]), *p0)
                    dve.sem_inc(base_set.sem, 1)
                    link(dve.tensor_tensor(scratch, dstf[:, :, :],
                                           base_f[:, :].unsqueeze(2).to_broadcast([P, NLX, T]), ALU.subtract), *p0)
                    link(dve.tensor_scalar(dl1[:, :, :], scratch, 1.0, None, ALU.add), *p0)
                    link(dve.tensor_tensor(sl1[:, :, :], dl1[:, :, :], loops[:, :, :], ALU.mult), *p0)
                    dve.tensor_tensor(sl1[:, :, :], sl1[:, :, :], lo1[:, :, :], ALU.add)
                    link(dve.scalar_tensor_tensor(inw, scratch, float(P) - 0.5, rem[:, :, :], ALU.is_lt, ALU.mult), *p0)
                    link(dve.scalar_tensor_tensor(khi[:, :, :], hi[:, :, :], 1.0, inw, ALU.add, ALU.mult), *p0)
                    for q in range(2):
                        deal_tiles(*p0, q)
                        deal_counts()
                        deal_scan(*p0, q)
                        deal_own_count(*p0)
                        deal_ranks(*p0, q)
                        deal_places(*p0, 0)
                        deal_places(*p0, 1)
                        deal_numbers()
                        deal_senders(q)
                        deal_receivers(q)
                        deal_keys(*p0, q, q, q)
                    with dve.Fori(0, BODIES) as i:
                        b0 = ("body", s, i)
                        onehots(s, i, 0)
                        low_part(s, i, 0)
                        for c in range(BC):
                            q, cc = c // NC_, c % NC_
                            if c > 0:
                                add_group(s, i, c - 1, 1)
                                low_part_h(s, i, c - 1)
                            if c + 1 < BC:
                                onehots(s, i, c + 1)
                            if cc > 0:
                                add_group(s, i, c - 1, 2)
                            if c + 1 < BC:
                                low_part(s, i, c + 1)
                            add_group(s, i, c, 0)
                            if c == NC_:
                                save_window(s, i, 0)
                            if c == BC - 1:
                                add_group(s, i, c, 1)
                                low_part_h(s, i, c)
                            nxt = i * 2 + (2 + q)
                            if cc == 0:
                                deal_tiles(*b0, nxt)
                            if cc == 1:
                                deal_counts()
                            if cc == 2:
                                deal_numbers()
                            if cc == 3:
                                deal_scan(*b0, 2 + q)
                            if cc == 4:
                                deal_own_count(*b0)
                                deal_senders(nxt)
                            if cc == 5:
                                deal_ranks(*b0, nxt)
                            if cc in (6, 7):
                                deal_places(*b0, cc - 6)
                            if cc == 8:
                                deal_receivers(nxt)
                            if cc == NC_ - 1:
                                wait(dve, gh_count[c % RG], s, i, 16 * CH * gh_use[c][0])
                                deal_keys(*b0, nxt, q, 2 + q)
                        save_window(s, i, 1)
                    e0 = ("end", s, 0)
                    dve.tensor_reduce(left[:, 0:1], rem[:, :, :].rearrange("p l t -> p (l t)"), AX, ALU.add)\
                        .then_inc(left_ready.sem, 1)
                    link(dve.tensor_scalar(swf[:, 0:1], swf[:, 0:1], 1.0, None, ALU.add), *e0)
                    link(dve.tensor_scalar(swf[:, 1:2], swf[:, 0:1], 1.0, None, ALU.add), *e0)
                    wait(dve, left_total, s, 0, 1)
                    link(dve.tensor_scalar(swf[:, 2:3], rb[0:1, 0:1], 0.5, None, ALU.is_gt), *e0)
                    link(dve.tensor_tensor(swf[:, 2:3], swf[:, 2:3], swf[:, 1:2], ALU.mult), *e0)
                    link(dve.tensor_copy(ctl[0:1, 0:1], swf[:, 2:3]), *e0)
                    link(dve.tensor_copy(ctl[0:1, 1:2], swf[:, 0:1]), *e0)
                    dve.sem_inc(sweep_end.sem, 1)
                    dve.load(end, ctl[0:1, 0:1])
                assert links == plan, links


        src_y = sb("src_y", [P, NB, D])
        y_tab = sb("y_tab", [P, NB, D])
        update_nodes(nc, sb, sem, bank, wt, bb, ident, table, y_tab, src_y, acc1_dram, x_rows, x_t, x1_dram, y_dram)
        sum_neighbours(nc, sb, sem, bank, iota_m, table, src_y, acc2_dram, y_dram, keys_dram, base_dram, ctl)
        finish_nodes(nc, sb, sem, bank, wt, bb, ident, src_sum, y_tab, src_y, acc1_dram, acc2_dram, x1_dram, out)


LINKS_PRO = 11 + 2 * 14
LINKS_BODY = 2 * 14
LINKS_END = 6
HALVES = ((0, 4), (4, 3))


class Turns:

    def __init__(self, sem, passed, names):
        self.sem, self.passed, self.names = sem, passed, names

    def value(self, e, name):
        return e * len(self.names) + (self.names.index(name) + 1)

    def wait_before(self, eng, e, name):
        eng.wait_ge(self.sem, self.value(e, name))
        eng.sem_inc(self.passed, 1)

    def wait_after(self, eng, e, name):
        eng.wait_ge(self.sem, e * len(self.names) + (self.names.index(name) + 2))
        eng.sem_inc(self.passed, 1)

    def wait_all(self, eng, e):
        eng.wait_ge(self.sem, e * len(self.names) + (len(self.names) + 1))
        eng.sem_inc(self.passed, 1)


def node_rows(dram, e, c0=0, c1=None):
    return dram[bass.ds(e * (KB * P), KB * P), c0:c1 or dram.shape[1]].rearrange("(k p) c -> p k c", p=P)


def transpose_blocks(pe, bank, src, ident):
    for h, (k0, kn) in enumerate(HALVES):
        for k in range(kn):
            last = pe.transpose(bank[1 + h][0:D, k * P:(k + 1) * P], src(k0 + k), ident[:, :])
    return last


def multiply_blocks(pe, bank, terms):
    for k in range(KB):
        for n, (lhs, weight) in enumerate(terms):
            last = pe.matmul(bank[0][:, k * D:(k + 1) * D], lhs[:, k * P:(k + 1) * P], weight,
                             start=(n == 0), stop=(n == len(terms) - 1))
    return last


def copy_blocks(dve, bank, dst):
    for h, (k0, kn) in enumerate(HALVES):
        last = dve.tensor_copy(dst[:, k0 * P:(k0 + kn) * P], bank[1 + h][0:D, 0:kn * P])
    return last


UPDATE_STEPS = ("sumh_t", "sumh_c", "msg", "cnt", "rcnt", "b2cnt", "num", "mean", "mean_t", "mean_c", "upd1",
                "pre", "silu", "hu_t", "hu_c", "upd2", "new", "res", "ln_sum", "ln_mean", "ln_cen", "ln_sq", "ln_var",
                "ln_eps", "ln_sqrt", "ln_rec", "ln_out", "x1_t", "x1_c", "y", "y_c", "y_tab",
                "y_1", "y_rest1", "y_2", "y_3", "y_parts")
FINISH_STEPS = ("both", "cnt", "cmax", "rcnt", "n2", "n2m", "n3", "n1_t", "n1_c", "n3_t", "n3_c", "emb",
                "b1cnt", "acc2", "srcy", "selfy", "sum", "relu", "relu_t", "relu_c", "n2_t", "n2_c", "out1",
                "o1", "x1_t", "x1_c", "out2", "bias", "o2", "res", "ln_sum", "ln_mean", "ln_cen", "ln_sq", "ln_var",
                "ln_eps", "ln_sqrt", "ln_rec", "ln_out")


def update_nodes(nc, sb, sem, bank, wt, bb, ident, table, y_tab, src_y, acc1_dram, x_rows, x_t, x1_dram, y_dram):
    with ExitStack() as cn:
        acc = sb("u_acc", [P, KB, G0], c=cn)
        xr = sb("u_xr", [P, KB, D], c=cn)
        xt = sb("u_xt", [D, KB * P], c=cn)
        yp = sb("u_yp", [P, KB, PARTS, D], BF16, c=cn)
        a, b, cen, sq, res = (sb(f"u_{n}", [P, KB, D], c=cn) for n in ("a", "b", "cen", "sq", "x1"))
        t1, t2 = (sb(f"u_{n}", [D, KB * P], c=cn) for n in ("t1", "t2"))
        sc = sb("u_sc", [P, 8, KB], c=cn)
        ps = bank[0][:, 0:KB * D].rearrange("p (k d) -> p k d", d=D)
        loaded, stored = sem("u_loaded"), sem("u_stored")
        turns = Turns(sem("u_step"), sem("u_pass"), UPDATE_STEPS)
        block = cn.enter_context(nc.Block())

        def broad(n):
            return bb[:, n:n + 1, :].to_broadcast([P, KB, D])

        def per_node(n):
            return sc[:, n, :].unsqueeze(2).to_broadcast([P, KB, D])

        @block.sync
        def _(sp):
            def load(e):
                sp.dma_start(acc[:, :, :], node_rows(acc1_dram, e, 0, G0)).then_inc(loaded, 16)
                sp.dma_start(xr[:, :, :], node_rows(x_rows, e)).then_inc(loaded, 16)
                sp.dma_start(xt[:, :], x_t[:, bass.ds(e * (KB * P), KB * P)]).then_inc(loaded, 16)

            def store(e):
                turns.wait_all(sp, e)
                sp.dma_start(node_rows(x1_dram, e), res[:, :, :]).then_inc(stored, 16)
                sp.dma_start(node_rows(y_dram, e), yp[:, :, :, :].rearrange("p k a d -> p k (a d)")).then_inc(stored, 16)
                sp.wait_ge(stored, e * 32 + 64)
                sp.sem_inc(turns.passed, 1)

            sp.sem_inc(turns.sem, 1)
            sp.sem_inc(stored, 32)
            load(0)
            with sp.Fori(0, NB // KB - 1) as e:
                turns.wait_after(sp, e, "res")
                load(e + 1)
                store(e)
            store(NB // KB - 1)

        @block.gpsimd
        def _(pool):
            pool.memset(src_y[:, :, :], 0.0).then_inc(turns.passed, 1)

        @block.tensor
        def _(pe):
            with pe.Fori(0, NB // KB) as e:
                pe.wait_ge(loaded, e * 48 + 48)
                turns.wait_before(pe, e, "sumh_t")
                transpose_blocks(pe, bank, lambda k: acc[:, k, 0:D], ident).then_inc(turns.sem, 1)
                turns.wait_before(pe, e, "msg")
                multiply_blocks(pe, bank, [(t1, wt(W2M))]).then_inc(turns.sem, 1)
                turns.wait_before(pe, e, "mean_t")
                transpose_blocks(pe, bank, lambda k: a[:, k, :], ident).then_inc(turns.sem, 1)
                turns.wait_before(pe, e, "upd1")
                multiply_blocks(pe, bank, [(xt, wt(U1A)), (t2, wt(U1B))]).then_inc(turns.sem, 1)
                turns.wait_before(pe, e, "hu_t")
                transpose_blocks(pe, bank, lambda k: b[:, k, :], ident).then_inc(turns.sem, 1)
                turns.wait_before(pe, e, "upd2")
                multiply_blocks(pe, bank, [(t1, wt(W2U))]).then_inc(turns.sem, 1)
                turns.wait_before(pe, e, "x1_t")
                transpose_blocks(pe, bank, lambda k: res[:, k, :], ident).then_inc(turns.sem, 1)
                turns.wait_before(pe, e, "y")
                multiply_blocks(pe, bank, [(t1, wt(V1A))]).then_inc(turns.sem, 1)

        @block.scalar
        def _(act):
            with act.Fori(0, NB // KB) as e:
                turns.wait_before(act, e, "silu")
                act.activation(b[:, :, :], a[:, :, :], ACT.Silu).then_inc(turns.sem, 1)
                turns.wait_before(act, e, "ln_sqrt")
                act.activation(sc[:, 4, :], sc[:, 3, :], ACT.Sqrt).then_inc(turns.sem, 1)

        @block.vector
        def _(dve):
            with dve.Fori(0, NB // KB) as e:
                def before(name):
                    turns.wait_before(dve, e, name)

                before("sumh_c")
                copy_blocks(dve, bank, t1).then_inc(turns.sem, 1)
                before("cnt")
                dve.tensor_scalar(sc[:, 0, :], acc[:, :, D], 1e-6, None, ALU.add).then_inc(turns.sem, 1)
                before("rcnt")
                dve.reciprocal(sc[:, 1, :], sc[:, 0, :]).then_inc(turns.sem, 1)
                before("b2cnt")
                dve.tensor_tensor(a[:, :, :], broad(B2M), acc[:, :, D:D + 1].to_broadcast([P, KB, D]),
                                  ALU.mult).then_inc(turns.sem, 1)
                before("num")
                dve.tensor_tensor(a[:, :, :], a[:, :, :], ps, ALU.add).then_inc(turns.sem, 1)
                before("mean")
                dve.tensor_tensor(a[:, :, :], a[:, :, :], per_node(1), ALU.mult).then_inc(turns.sem, 1)
                before("mean_c")
                copy_blocks(dve, bank, t2).then_inc(turns.sem, 1)
                before("pre")
                dve.tensor_tensor(a[:, :, :], ps, broad(B1U), ALU.add).then_inc(turns.sem, 1)
                before("hu_c")
                copy_blocks(dve, bank, t1).then_inc(turns.sem, 1)
                before("new")
                dve.tensor_tensor(b[:, :, :], ps, broad(B2U), ALU.add).then_inc(turns.sem, 1)
                before("res")
                dve.tensor_tensor(b[:, :, :], b[:, :, :], xr[:, :, :], ALU.add).then_inc(turns.sem, 1)
                layernorm_steps(dve, before, turns, b, cen, sq, sc, per_node, res, (stored, e * 32 + 32))
                before("x1_c")
                copy_blocks(dve, bank, t1).then_inc(turns.sem, 1)
                before("y_c")
                dve.tensor_copy(a[:, :, :], ps).then_inc(turns.sem, 1)
                before("y_tab")
                dve.tensor_scalar(y_tab[:, bass.ds(e * KB, KB), :], a[:, :, :], 1.0, None, ALU.mult)\
                    .then_inc(turns.sem, 1)
                before("y_1")
                dve.tensor_copy(yp[:, :, 0, :], a[:, :, :]).then_inc(turns.sem, 1)
                before("y_rest1")
                dve.tensor_tensor(a[:, :, :], a[:, :, :], yp[:, :, 0, :], ALU.subtract).then_inc(turns.sem, 1)
                before("y_2")
                dve.tensor_copy(yp[:, :, 1, :], a[:, :, :]).then_inc(turns.sem, 1)
                before("y_3")
                dve.tensor_tensor(yp[:, :, 2, :], a[:, :, :], yp[:, :, 1, :], ALU.subtract).then_inc(turns.sem, 1)
                before("y_parts")
                dve.tensor_scalar(table[:, bass.ds(e * KB, KB), :, :].rearrange("p k a d -> p k (a d)"),
                                  yp[:, :, :, :].rearrange("p k a d -> p k (a d)"), 1.0, None, ALU.mult)\
                    .then_inc(turns.sem, 1)


def layernorm_steps(dve, before, turns, b, cen, sq, sc, per_node, res, last_stored):
    before("ln_sum")
    dve.tensor_reduce(sc[:, 2, :], b[:, :, :], AX, ALU.add).then_inc(turns.sem, 1)
    before("ln_mean")
    dve.tensor_scalar(sc[:, 5, :], sc[:, 2, :], 1.0 / D, None, ALU.mult).then_inc(turns.sem, 1)
    before("ln_cen")
    dve.tensor_tensor(cen[:, :, :], b[:, :, :], per_node(5), ALU.subtract).then_inc(turns.sem, 1)
    before("ln_sq")
    dve.tensor_tensor(sq[:, :, :], cen[:, :, :], cen[:, :, :], ALU.mult).then_inc(turns.sem, 1)
    before("ln_var")
    dve.tensor_reduce(sc[:, 6, :], sq[:, :, :], AX, ALU.add).then_inc(turns.sem, 1)
    before("ln_eps")
    dve.tensor_scalar(sc[:, 3, :], sc[:, 6, :], 1.0 / D, 1e-5, ALU.mult, ALU.add).then_inc(turns.sem, 1)
    before("ln_rec")
    dve.reciprocal(sc[:, 7, :], sc[:, 4, :]).then_inc(turns.sem, 1)
    before("ln_out")
    dve.wait_ge(*last_stored)
    dve.sem_inc(turns.passed, 1)
    dve.tensor_tensor(res[:, :, :], cen[:, :, :], per_node(7), ALU.mult).then_inc(turns.sem, 1)


def finish_nodes(nc, sb, sem, bank, wt, bb, ident, src_sum, y_tab, src_y, acc1_dram, acc2_dram, x1_dram, out):
    with ExitStack() as cn:
        acc = sb("f_acc", [P, KB, W], c=cn)
        tot = sb("f_tot", [P, KB, W], c=cn)
        xr = sb("f_xr", [P, KB, D], c=cn)
        acc2 = sb("f_acc2", [P, KB, D], c=cn)
        a, b, cen, sq, res = (sb(f"f_{n}", [P, KB, D], c=cn) for n in ("a", "b", "cen", "sq", "res"))
        t1, t2 = (sb(f"f_{n}", [D, KB * P], c=cn) for n in ("t1", "t2"))
        sc = sb("f_sc", [P, 8, KB], c=cn)
        sd = sb("f_sd", [P, 2, KB], c=cn)
        ps = bank[0][:, 0:KB * D].rearrange("p (k d) -> p k d", d=D)
        loaded, stored = sem("f_loaded"), sem("f_stored")
        turns = Turns(sem("f_step"), sem("f_pass"), FINISH_STEPS)
        block = cn.enter_context(nc.Block())

        def broad(n):
            return bb[:, n:n + 1, :].to_broadcast([P, KB, D])

        def per_node(n):
            return sc[:, n, :].unsqueeze(2).to_broadcast([P, KB, D])

        @block.sync
        def _(sp):
            def load(e):
                sp.dma_start(acc[:, :, :], node_rows(acc1_dram, e, G0, WH)).then_inc(loaded, 16)
                sp.dma_start(acc2[:, :, :], node_rows(acc2_dram, e)).then_inc(loaded, 16)
                sp.dma_start(xr[:, :, :], node_rows(x1_dram, e)).then_inc(loaded, 16)

            def store(e):
                turns.wait_all(sp, e)
                sp.dma_start(node_rows(out, e), res[:, :, :]).then_inc(stored, 16)
                sp.wait_ge(stored, e * 16 + 32)
                sp.sem_inc(turns.passed, 1)

            sp.sem_inc(turns.sem, 1)
            sp.sem_inc(stored, 16)
            load(0)
            with sp.Fori(0, NB // KB - 1) as e:
                turns.wait_after(sp, e, "res")
                load(e + 1)
                store(e)
            store(NB // KB - 1)

        @block.tensor
        def _(pe):
            with pe.Fori(0, NB // KB) as e:
                turns.wait_before(pe, e, "n1_t")
                transpose_blocks(pe, bank, lambda k: tot[:, k, 0:D], ident).then_inc(turns.sem, 1)
                turns.wait_before(pe, e, "n3_t")
                transpose_blocks(pe, bank, lambda k: tot[:, k, 2 * D:3 * D], ident).then_inc(turns.sem, 1)
                turns.wait_before(pe, e, "emb")
                multiply_blocks(pe, bank, [(t1, wt(V1B)), (t2, wt(V1C))]).then_inc(turns.sem, 1)
                turns.wait_before(pe, e, "relu_t")
                transpose_blocks(pe, bank, lambda k: b[:, k, :], ident).then_inc(turns.sem, 1)
                turns.wait_before(pe, e, "n2_t")
                transpose_blocks(pe, bank, lambda k: tot[:, k, D:2 * D], ident).then_inc(turns.sem, 1)
                turns.wait_before(pe, e, "out1")
                multiply_blocks(pe, bank, [(t1, wt(Z2A)), (t2, wt(Z2C))]).then_inc(turns.sem, 1)
                turns.wait_before(pe, e, "x1_t")
                transpose_blocks(pe, bank, lambda k: xr[:, k, :], ident).then_inc(turns.sem, 1)
                turns.wait_before(pe, e, "out2")
                multiply_blocks(pe, bank, [(t1, wt(Z2B))]).then_inc(turns.sem, 1)

        @block.scalar
        def _(act):
            with act.Fori(0, NB // KB) as e:
                turns.wait_before(act, e, "ln_sqrt")
                act.activation(sc[:, 4, :], sc[:, 3, :], ACT.Sqrt).then_inc(turns.sem, 1)

        @block.vector
        def _(dve):
            with dve.Fori(0, NB // KB) as e:
                def before(name):
                    turns.wait_before(dve, e, name)

                def tt(name, o, x, y, op):
                    before(name)
                    dve.tensor_tensor(o, x, y, op).then_inc(turns.sem, 1)

                n2, n3 = tot[:, :, D:2 * D], tot[:, :, 2 * D:3 * D]
                dve.wait_ge(loaded, e * 48 + 48)
                tt("both", tot[:, :, :], acc[:, :, :], src_sum[:, bass.ds(e * KB, KB), :], ALU.add)
                before("cnt")
                dve.tensor_scalar(sc[:, 0, :], tot[:, :, W - 2], 1.0, None, ALU.add).then_inc(turns.sem, 1)
                before("cmax")
                dve.tensor_scalar(sd[:, 0, :], sc[:, 0, :], 1.0, None, ALU.max).then_inc(turns.sem, 1)
                before("rcnt")
                dve.reciprocal(sc[:, 1, :], sd[:, 0, :]).then_inc(turns.sem, 1)
                tt("n2", n2, n2, broad(TU), ALU.add)
                tt("n2m", n2, n2, per_node(1), ALU.mult)
                tt("n3", n3, n3, broad(TU), ALU.add)
                before("n1_c")
                copy_blocks(dve, bank, t1).then_inc(turns.sem, 1)
                before("n3_c")
                copy_blocks(dve, bank, t2).then_inc(turns.sem, 1)
                tt("b1cnt", a[:, :, :], broad(C1), per_node(0), ALU.mult)
                tt("acc2", a[:, :, :], a[:, :, :], acc2[:, :, :], ALU.add)
                tt("srcy", a[:, :, :], a[:, :, :], src_y[:, bass.ds(e * KB, KB), :], ALU.add)
                tt("selfy", a[:, :, :], a[:, :, :], y_tab[:, bass.ds(e * KB, KB), :], ALU.add)
                tt("sum", a[:, :, :], a[:, :, :], ps, ALU.add)
                before("relu")
                dve.tensor_scalar(b[:, :, :], a[:, :, :], 0.0, None, ALU.max).then_inc(turns.sem, 1)
                before("relu_c")
                copy_blocks(dve, bank, t1).then_inc(turns.sem, 1)
                before("n2_c")
                copy_blocks(dve, bank, t2).then_inc(turns.sem, 1)
                before("o1")
                dve.tensor_copy(a[:, :, :], ps).then_inc(turns.sem, 1)
                before("x1_c")
                copy_blocks(dve, bank, t1).then_inc(turns.sem, 1)
                tt("bias", b[:, :, :], ps, broad(C2), ALU.add)
                tt("o2", a[:, :, :], a[:, :, :], b[:, :, :], ALU.add)
                tt("res", b[:, :, :], a[:, :, :], xr[:, :, :], ALU.add)
                layernorm_steps(dve, before, turns, b, cen, sq, sc, per_node, res, (stored, e * 16 + 16))


def sum_neighbours(nc, sb, sem, bank, iota_m, table, src_y, acc2_dram, y_dram, keys_dram, base_dram, ctl):
    RO2, RA = 4, 4
    with ExitStack() as c3:
        oh = sb("n_oh", [P, RO2, 2, CH, P], BF16, c=c3)
        adj = sb("n_adj", [P, RA, 4 * P], BF16, c=c3)
        keys = sb("n_keys", [P, 2, 2, NT], BF16, c=c3)
        yw = sb("n_yw", [P, 2, PARTS, D], BF16, c=c3)
        base = sb("n_base", [1, MAXSW * NL], I32, c=c3)
        dwin = sb("n_dwin", [P, 2, D], c=c3)
        unread = sb("n_unread", [P, 2, D3], BF16, c=c3)
        iob = sb("n_iob", [P, P], BF16, c=c3)
        adj_bank = [bank[0], bank[1], bank[2], bank[3]]
        srcb, dstb = [bank[4], bank[5]], bank[6]
        passed = sem("n_pass")
        consts = sem("n_consts")
        base_loaded = sem("n_base_loaded")
        keys_loaded = [Count(sem(f"n_keys_loaded{q}"), 16) for q in range(2)]
        yw_loaded = [Count(sem(f"n_yw_loaded{q}"), 16) for q in range(2)]
        oh_ready = Count(sem("n_oh_ready"), BC)
        adj_done = Count(sem("n_adj_done"), BC * NG)
        adj_copied = Count(sem("n_adj_copied"), BC * NG, credit=RA)
        adj_used = Count(sem("n_adj_used"), BC * (NG - 1), credit=RA)
        src_ready = Count(sem("n_src_ready"), BC, credit=BC)
        src_added = Count(sem("n_src_added"), BC, credit=4)
        dwin_saved = Count(sem("n_dwin_saved"), 2, credit=4)
        dwin_added = Count(sem("n_dwin_added"), 32, credit=32)
        block = c3.enter_context(nc.Block())

        def wait(eng, cnt, s, i, n):
            eng.wait_ge(cnt.sem, cnt.at(s, i, n))

        def hold(eng, cnt, s, i, n):
            wait(eng, cnt, s, i, n)
            eng.sem_inc(passed, 1)

        def sweep_count(eng, name):
            end = eng.alloc_register(name)
            eng.load(end, ctl[0:1, 1:2])
            return end

        @block.sync
        def _(sp):
            end = sweep_count(sp, "n_end_sp")
            for cnt in (adj_copied, adj_used, src_ready, src_added, dwin_saved):
                sp.sem_inc(cnt.sem, cnt.credit)
            with sp.Fori(0, end) as s:
                sp.dma_start(base[0:1, bass.ds(s * NL, NL)], base_dram[bass.ds(s, 1), :]).then_inc(base_loaded, 16)
                sp.wait_ge(base_loaded, s * 16 + 16)
                sp.sem_inc(passed, 1)
                with sp.Fori(0, BODIES) as i:
                    for q in range(2):
                        b = sp.value_load(base[0:1, bass.ds(s * NL + i * 2 + q, 1)], min_val=0, max_val=N - 1)
                        hold(sp, src_ready, s, i, NC_ * (q + 1) - BC)
                        sp.dma_start(yw[:, q, :, :].rearrange("p a d -> p (a d)"), y_dram[bass.ds(b, P), :]).then_inc(yw_loaded[q].sem, 16)
                        sp.dma_start(keys[:, q, :, :].rearrange("p a b -> p (a b)"),
                                     keys_dram[bass.ds((s * NL + i * 2 + q) * P, P), :])\
                            .then_inc(keys_loaded[q].sem, 16)

        @block.gpsimd
        def _(pool):
            end = sweep_count(pool, "n_end_pool")
            for r in range(2):
                pool.dma_start(unread[:, r, :], y_dram[0:P, :]).then_inc(dwin_added.sem, 16)
                pool.wait_ge(dwin_added.sem, 16 * (r + 1))
            with pool.Fori(0, end) as s:
                pool.wait_ge(base_loaded, s * 16 + 16)
                pool.sem_inc(passed, 1)
                with pool.Fori(0, BODIES) as i:
                    for q in range(2):
                        b = pool.value_load(base[0:1, bass.ds(s * NL + i * 2 + q, 1)], min_val=0, max_val=N - 1)
                        hold(pool, dwin_saved, s, i, q + 1)
                        hold(pool, dwin_added, s, i, 16 * q)
                        pool.dma_start(acc2_dram[bass.ds(b, P), :], dwin[:, q, :],
                                       accum_op=ALU.add).then_inc(dwin_added.sem, 16)
                hold(pool, dwin_added, s, BODIES, 0)

        @block.scalar
        def _(act):
            end = sweep_count(act, "n_end_act")
            with act.Fori(0, end) as s:
                with act.Fori(0, BODIES) as i:
                    for c in range(BC):
                        for g, (k0, kn) in enumerate(GROUPS):
                            n = c * NG + g
                            before, (cu, gu) = (n < RA), divmod((n - RA) % (BC * NG), NG)
                            if gu == NG - 1:
                                wait(act, src_ready, s, i, cu + 1 - before * BC)
                            else:
                                wait(act, adj_used, s, i, (cu - before * BC) * (NG - 1) + gu + 1)
                            wait(act, adj_done, s, i, n + 1)
                            act.activation(adj[:, n % RA, 0:2 * kn * P], adj_bank[n % 4][:, 0:2 * kn * P], ACT.Copy)\
                                .then_inc(adj_copied.sem, 1)
                act.sem_inc(passed, 1)

        @block.tensor
        def _(pe):
            end = sweep_count(pe, "n_end_pe")
            with pe.Fori(0, end) as s:
                with pe.Fori(0, BODIES) as i:
                    def adjacency(n):
                        c, g = n // NG, n % NG
                        k0, kn = GROUPS[g]
                        if g == 0:
                            wait(pe, oh_ready, s, i, c + 1)
                        wait(pe, adj_copied, s, i, n + 1 - 4)
                        for k in range(kn):
                            snd, rcv = oh[:, c % RO2, 0, k0 + k, :], oh[:, c % RO2, 1, k0 + k, :]
                            for m, (x, y) in enumerate(((snd, rcv), (rcv, snd))):
                                last = pe.matmul(adj_bank[n % 4][:, (2 * k + m) * P:(2 * k + m + 1) * P], x, y,
                                                 start=True, stop=True)
                        last.then_inc(adj_done.sem, 1)

                    def sums(n):
                        c, g = n // NG, n % NG
                        q, cc = c // NC_, c % NC_
                        k0, kn = GROUPS[g]
                        if g == 0:
                            wait(pe, src_added, s, i, c - 1)
                        if g == 0 and cc == 0:
                            wait(pe, yw_loaded[q], s, i, 16)
                            wait(pe, dwin_saved, s, i, q)
                        wait(pe, adj_copied, s, i, n + 1)
                        for k in range(kn):
                            t = k0 + k
                            b = cc * CH + t
                            to_rcv, to_snd = adj[:, n % RA, 2 * k * P:(2 * k + 1) * P], \
                                adj[:, n % RA, (2 * k + 1) * P:(2 * k + 2) * P]
                            for a in range(PARTS):
                                y = yw[:, q, a, :] if b == SELF else table[:, b, a, :]
                                pe.matmul(dstb[:, 0:D], to_rcv, y, start=(b == 0 and a == 0), stop=False)
                            for a in range(PARTS):
                                if b == SELF:
                                    last = pe.matmul(dstb[:, 0:D], to_snd, yw[:, q, a, :],
                                                     start=False, stop=(a == PARTS - 1))
                                else:
                                    last = pe.matmul(srcb[c % 2][:, t * D:(t + 1) * D], to_snd, yw[:, q, a, :],
                                                     start=(a == 0), stop=(a == PARTS - 1))
                        if g < NG - 1:
                            last.then_inc(adj_used.sem, 1)
                        if g == NG - 1:
                            last.then_inc(src_ready.sem, 1)

                    for n in range(BC * NG + 2):
                        if n < BC * NG:
                            adjacency(n)
                        if n >= 2:
                            sums(n - 2)
                pe.sem_inc(passed, 1)

        @block.vector
        def _(dve):
            end = sweep_count(dve, "n_end_dve")
            dve.tensor_copy(iob[:, :], iota_m[:, :]).then_inc(consts, 1)
            dve.wait_ge(consts, 1)
            with dve.Fori(0, end) as s:
                with dve.Fori(0, BODIES) as i:
                    def onehots(c):
                        q, b0 = c // NC_, c % NC_ * CH
                        if c % NC_ == 0:
                            wait(dve, keys_loaded[q], s, i, 16)
                        wait(dve, src_ready, s, i, c + 1 - RO2)
                        for m in range(2):
                            last = dve.tensor_tensor(oh[:, c % RO2, m, :, :],
                                                     keys[:, q, m, b0:b0 + CH].unsqueeze(2).to_broadcast([P, CH, P]),
                                                     iob[:, :].unsqueeze(1).to_broadcast([P, CH, P]), ALU.is_equal)
                        last.then_inc(oh_ready.sem, 1)

                    onehots(0)
                    onehots(1)
                    for c in range(BC):
                        q, b0 = c // NC_, c % NC_ * CH
                        if c + 2 < BC:
                            onehots(c + 2)
                        wait(dve, src_ready, s, i, c + 1)
                        kn = min(CH, NB - b0)
                        dve.tensor_tensor(src_y[:, b0:b0 + kn, :], src_y[:, b0:b0 + kn, :],
                                          srcb[c % 2][:, 0:kn * D].rearrange("p (k d) -> p k d", d=D),
                                          ALU.add).then_inc(src_added.sem, 1)
                        if c % NC_ == NC_ - 1:
                            hold(dve, dwin_added, s, i, 16 * q - 16)
                            dve.tensor_copy(dwin[:, q, :], dstb[:, 0:D]).then_inc(dwin_saved.sem, 1)
                dve.sem_inc(passed, 1)


def kernel(**inputs):
    import concourse.bacc as _bacc
    from concourse.bass_utils import run_bass_kernel_spmd as _run

    inp = {k: np.asarray(v) for k, v in inputs.items()}
    pad = NLX * LOT - E
    src = np.concatenate([inp["src"], np.full(pad, NB * P, inp["src"].dtype)])
    dst = np.pad(inp["dst"], (0, pad), mode="edge")

    def lots(v):
        return np.ascontiguousarray(v.reshape(NLX, P, T).transpose(1, 0, 2).reshape(P, NLX * T))

    x = np.concatenate([inp["x"], np.zeros((NROWS - N, D), inp["x"].dtype)])
    wm, wu, v1, z2 = inp["L0_gnn_W1_msg"], inp["L0_gnn_W1_upd"], inp["L1_gnn_W1"], inp["L1_gnn_W2"]
    blocks = [wm[0:D], wm[D:2 * D], wm[2 * D:], inp["L0_gnn_W2_msg"], wu[0:D], wu[D:], inp["L0_gnn_W2_upd"],
              v1[:, 0:D].T, v1[:, D:2 * D].T, v1[:, 2 * D:].T, z2[:, 0:D].T, z2[:, D:2 * D].T, z2[:, 2 * D:].T]
    rows = [inp["L0_gnn_b1_msg"], inp["L0_gnn_b2_msg"], inp["L0_gnn_b1_upd"], inp["L0_gnn_b2_upd"],
            inp["L1_gnn_b1"], inp["L1_gnn_b2"], inp["edge_attr_64_n2"][0]]
    arrays = {
        "edges": np.ascontiguousarray(np.concatenate(
            [inp["edge_attr_64"], inp["edge_attr_64_n2"], inp["edge_attr_64_n3"]], axis=1)),
        "src_t": lots(src), "dst_t": lots(dst), "x_t": np.ascontiguousarray(x.T), "x_rows": x,
        "wts": np.ascontiguousarray(np.concatenate(blocks, axis=1)),
        "bias": np.ascontiguousarray(np.concatenate(rows)[None]),
    }
    nc = _bacc.Bacc("TRN2", target_bir_lowering=False, num_devices=1)
    args = [nc.dram_tensor(k, a.shape, mybir.dt.from_np(a.dtype), kind="ExternalInput").ap() for k, a in arrays.items()]
    out = nc.dram_tensor("out", (NB * P, D), F32, kind="ExternalOutput").ap()
    gnn_kernel(nc, *args, out)
    r = _run(nc, [arrays], core_ids=[0])
    return r.results[0]["out"][:N]
```
